# Optimizing a Trainium2 kernel written in Bass

```python
import numpy as np
import jax
import jax.numpy as jnp

def _softmax(x, axis=-1):
    return jax.nn.softmax(x, axis=axis)

def _gelu(x):
    return jax.nn.gelu(x, approximate=True)

def _silu(x):
    return jax.nn.silu(x)

def _sigmoid(x):
    return jax.nn.sigmoid(x)

def _layernorm(x, axis=-1, eps=1e-05):
    m = jnp.mean(x, axis=axis, keepdims=True)
    v = jnp.var(x, axis=axis, keepdims=True)
    return (x - m) / jnp.sqrt(v + eps)

def _scatter_add(tgt, idx, src, axis=0):
    return tgt.at[idx].add(src)

def _segment_sum(src, seg, n):
    return jax.ops.segment_sum(src, seg, n)
kernel_name = 'mk_gnn_resnorm_d2_gnn_r8_694f30'

def setup_inputs(seed: int=0):
    np.random.seed(seed)
    _w = jnp.asarray

    def _rec_inputs():
        import jax
        import jax.numpy as jnp
        _gk = jax.random.key(seed)
        x = -0.0003195 + 1 * jax.random.normal(jax.random.fold_in(_gk, 1), (6250, 160), jnp.float32)
        _s = jax.random.randint(jax.random.fold_in(_gk, 2), (100000,), 0, 6250, jnp.int32)
        _d = jax.random.randint(jax.random.fold_in(_gk, 3), (100000,), 0, 6250, jnp.int32)
        _loop = jnp.arange(6250, dtype=jnp.int32)
        src = jnp.concatenate([_s, _d, _loop])
        dst = jnp.concatenate([_d, _s, _loop])
        _o = jnp.argsort(dst, stable=True)
        src = src[_o]
        dst = dst[_o]
        edge_attr_16 = 6.40344e-05 + 1.00026 * jax.random.normal(jax.random.fold_in(_gk, 12), (206250, 16), jnp.float32)
        edge_attr_4 = 0.000714719 + 1.00021 * jax.random.normal(jax.random.fold_in(_gk, 13), (206250, 4), jnp.float32)
        node_vec1 = jax.random.uniform(jax.random.fold_in(_gk, 15), (6250, 1), jnp.float32, 0.0, 1)
        return (x, src, dst, edge_attr_16, edge_attr_4, node_vec1)
    x, src, dst, edge_attr_16, edge_attr_4, node_vec1 = _rec_inputs()

    def _L0_gnn_setup():
        import jax, jax.numpy as jnp
        import numpy as np
        N_NODES = 12500
        N_EDGES = 100000
        MUL_S = 64
        MUL_V = 32
        DIM = MUL_S + 3 * MUL_V
        EDGE_SCALAR_DIM = 16
        ISQ3 = 1.0 / np.sqrt(3.0)
        ISQ2 = 1.0 / np.sqrt(2.0)

        def _forward(x, edge_index, edge_feat, edge_scalars, W_ss, W_sv, W_vs, W_vv, W_rad, b_rad, L_s, L_v):
            src, dst = (edge_index[0], edge_index[1])
            n = x.shape[0]
            xs = x[:, :MUL_S]
            xv = x[:, MUL_S:].reshape(n, MUL_V, 3)
            xs_e = xs[src]
            xv_e = xv[src]
            es = edge_feat[:, 0]
            ev = edge_feat[:, 1:4]
            out_s = (jnp.einsum('eu,uo->eo', xs_e * es[:, None], W_ss) / np.sqrt(MUL_S) + jnp.einsum('eud,ed,uo->eo', xv_e, ev, W_vv) * ISQ3 / np.sqrt(MUL_V)) * ISQ2
            out_v = (jnp.einsum('eu,ed,uv->evd', xs_e, ev, W_sv) * ISQ3 / np.sqrt(MUL_S) + jnp.einsum('eud,e,uv->evd', xv_e, es, W_vs) * ISQ3 / np.sqrt(MUL_V)) * ISQ2
            messages = jnp.concatenate([out_s, out_v.reshape(-1, 3 * MUL_V)], axis=1)
            scale = jax.nn.sigmoid(edge_scalars @ W_rad.T + b_rad)
            messages = messages * scale
            agg = jax.ops.segment_sum(messages, dst, num_segments=n)
            h = x + agg
            hs = h[:, :MUL_S]
            hv = h[:, MUL_S:].reshape(n, MUL_V, 3)
            ys = hs @ L_s / np.sqrt(MUL_S)
            yv = jnp.einsum('nud,uv->nvd', hv, L_v) / np.sqrt(MUL_V)
            return jnp.concatenate([ys, yv.reshape(n, 3 * MUL_V)], axis=1)
        key = jax.random.key(seed)
        ks = jax.random.split(key, 12)
        x = jax.random.normal(ks[0], (N_NODES, DIM), dtype=jnp.float32)
        edge_index = jax.random.randint(ks[1], (2, N_EDGES), 0, N_NODES, dtype=jnp.int64)
        edge_feat = jax.random.normal(ks[2], (N_EDGES, 4), dtype=jnp.float32)
        edge_scalars = jax.random.normal(ks[3], (N_EDGES, EDGE_SCALAR_DIM), dtype=jnp.float32)
        W_ss = jax.random.normal(ks[4], (MUL_S, MUL_S), dtype=jnp.float32)
        W_sv = jax.random.normal(ks[5], (MUL_S, MUL_V), dtype=jnp.float32)
        W_vs = jax.random.normal(ks[6], (MUL_V, MUL_V), dtype=jnp.float32)
        W_vv = jax.random.normal(ks[7], (MUL_V, MUL_S), dtype=jnp.float32)
        W_rad = jax.random.normal(ks[8], (DIM, EDGE_SCALAR_DIM), dtype=jnp.float32) / np.sqrt(EDGE_SCALAR_DIM)
        b_rad = jax.random.normal(ks[9], (DIM,), dtype=jnp.float32) * 0.1
        L_s = jax.random.normal(ks[10], (MUL_S, MUL_S), dtype=jnp.float32)
        L_v = jax.random.normal(ks[11], (MUL_V, MUL_V), dtype=jnp.float32)
        return {'x': x, 'edge_index': edge_index, 'edge_feat': edge_feat, 'edge_scalars': edge_scalars, 'W_ss': W_ss, 'W_sv': W_sv, 'W_vs': W_vs, 'W_vv': W_vv, 'W_rad': W_rad, 'b_rad': b_rad, 'L_s': L_s, 'L_v': L_v}
    _L0_gnn_all = _L0_gnn_setup()
    _L0_gnn_in = {k: v for k, v in _L0_gnn_all.items() if k in ('W_ss', 'W_sv', 'W_vs', 'W_vv', 'W_rad', 'b_rad', 'L_s', 'L_v')}
    del _L0_gnn_all

    def _L1_gnn_setup():
        import jax, jax.numpy as jnp
        import numpy as np
        N = 2500
        E = 40000
        MUL0 = 64
        MUL1 = 32
        FC_IN = 16
        FC_H = 64
        WNUM = 192
        key = jax.random.key(seed)
        ks = jax.random.split(key, 16)
        return {'x': jax.random.normal(ks[0], (N, MUL0 + 3 * MUL1), jnp.float32), 'node_attr': jnp.ones((N, 1), jnp.float32), 'edge_scalars': jax.random.normal(ks[1], (E, FC_IN), jnp.float32), 'edge_attr_sh': jax.random.normal(ks[2], (E, 4), jnp.float32), 'edge_src': jax.random.randint(ks[3], (E,), 0, N), 'edge_dst': jax.random.randint(ks[4], (E,), 0, N), 'Wfc1': jax.random.normal(ks[5], (FC_IN, FC_H), jnp.float32), 'Wfc2': jax.random.normal(ks[6], (FC_H, WNUM), jnp.float32), 'Wsc0': jax.random.normal(ks[7], (MUL0, MUL0), jnp.float32), 'Wsc1': jax.random.normal(ks[8], (MUL1, MUL1), jnp.float32), 'Wl1_0': jax.random.normal(ks[9], (MUL0, MUL0), jnp.float32), 'Wl1_1': jax.random.normal(ks[10], (MUL1, MUL1), jnp.float32), 'Wl2_s': jax.random.normal(ks[11], (MUL0 + MUL1, MUL0), jnp.float32), 'Wl2_v': jax.random.normal(ks[12], (MUL0 + MUL1, MUL1), jnp.float32), 'Wa': 0.1 * jax.random.normal(ks[13], (MUL0 + MUL1, 1), jnp.float32)}
    _L1_gnn_all = _L1_gnn_setup()
    _L1_gnn_in = {k: v for k, v in _L1_gnn_all.items() if k in ('Wfc1', 'Wfc2', 'Wsc0', 'Wsc1', 'Wl1_0', 'Wl1_1', 'Wl2_s', 'Wl2_v', 'Wa')}
    del _L1_gnn_all
    return {'x': x, 'src': src, 'dst': dst, 'edge_attr_16': edge_attr_16, 'edge_attr_4': edge_attr_4, 'node_vec1': node_vec1, 'L0_gnn_W_ss': _L0_gnn_in['W_ss'], 'L0_gnn_W_sv': _L0_gnn_in['W_sv'], 'L0_gnn_W_vs': _L0_gnn_in['W_vs'], 'L0_gnn_W_vv': _L0_gnn_in['W_vv'], 'L0_gnn_W_rad': _L0_gnn_in['W_rad'], 'L0_gnn_b_rad': _L0_gnn_in['b_rad'], 'L0_gnn_L_s': _L0_gnn_in['L_s'], 'L0_gnn_L_v': _L0_gnn_in['L_v'], 'L1_gnn_Wfc1': _L1_gnn_in['Wfc1'], 'L1_gnn_Wfc2': _L1_gnn_in['Wfc2'], 'L1_gnn_Wsc0': _L1_gnn_in['Wsc0'], 'L1_gnn_Wsc1': _L1_gnn_in['Wsc1'], 'L1_gnn_Wl1_0': _L1_gnn_in['Wl1_0'], 'L1_gnn_Wl1_1': _L1_gnn_in['Wl1_1'], 'L1_gnn_Wl2_s': _L1_gnn_in['Wl2_s'], 'L1_gnn_Wl2_v': _L1_gnn_in['Wl2_v'], 'L1_gnn_Wa': _L1_gnn_in['Wa']}

def reference(x, src, dst, edge_attr_16, edge_attr_4, node_vec1, L0_gnn_W_ss, L0_gnn_W_sv, L0_gnn_W_vs, L0_gnn_W_vv, L0_gnn_W_rad, L0_gnn_b_rad, L0_gnn_L_s, L0_gnn_L_v, L1_gnn_Wfc1, L1_gnn_Wfc2, L1_gnn_Wsc0, L1_gnn_Wsc1, L1_gnn_Wl1_0, L1_gnn_Wl1_1, L1_gnn_Wl2_s, L1_gnn_Wl2_v, L1_gnn_Wa):
    import jax
    import jax.numpy as jnp

    def _L0_gnn_ref(x, edge_index, edge_feat, edge_scalars, W_ss, W_sv, W_vs, W_vv, W_rad, b_rad, L_s, L_v):
        import jax, jax.numpy as jnp
        import numpy as np
        N_NODES = 12500
        N_EDGES = 100000
        MUL_S = 64
        MUL_V = 32
        DIM = MUL_S + 3 * MUL_V
        EDGE_SCALAR_DIM = 16
        ISQ3 = 1.0 / np.sqrt(3.0)
        ISQ2 = 1.0 / np.sqrt(2.0)

        def _forward(x, edge_index, edge_feat, edge_scalars, W_ss, W_sv, W_vs, W_vv, W_rad, b_rad, L_s, L_v):
            src, dst = (edge_index[0], edge_index[1])
            n = x.shape[0]
            xs = x[:, :MUL_S]
            xv = x[:, MUL_S:].reshape(n, MUL_V, 3)
            xs_e = xs[src]
            xv_e = xv[src]
            es = edge_feat[:, 0]
            ev = edge_feat[:, 1:4]
            out_s = (jnp.einsum('eu,uo->eo', xs_e * es[:, None], W_ss) / np.sqrt(MUL_S) + jnp.einsum('eud,ed,uo->eo', xv_e, ev, W_vv) * ISQ3 / np.sqrt(MUL_V)) * ISQ2
            out_v = (jnp.einsum('eu,ed,uv->evd', xs_e, ev, W_sv) * ISQ3 / np.sqrt(MUL_S) + jnp.einsum('eud,e,uv->evd', xv_e, es, W_vs) * ISQ3 / np.sqrt(MUL_V)) * ISQ2
            messages = jnp.concatenate([out_s, out_v.reshape(-1, 3 * MUL_V)], axis=1)
            scale = jax.nn.sigmoid(edge_scalars @ W_rad.T + b_rad)
            messages = messages * scale
            agg = jax.ops.segment_sum(messages, dst, num_segments=n)
            h = x + agg
            hs = h[:, :MUL_S]
            hv = h[:, MUL_S:].reshape(n, MUL_V, 3)
            ys = hs @ L_s / np.sqrt(MUL_S)
            yv = jnp.einsum('nud,uv->nvd', hv, L_v) / np.sqrt(MUL_V)
            return jnp.concatenate([ys, yv.reshape(n, 3 * MUL_V)], axis=1)
        return _forward(x, edge_index, edge_feat, edge_scalars, W_ss, W_sv, W_vs, W_vv, W_rad, b_rad, L_s, L_v)

    def _L1_gnn_ref(x, node_attr, edge_scalars, edge_attr_sh, edge_src, edge_dst, Wfc1, Wfc2, Wsc0, Wsc1, Wl1_0, Wl1_1, Wl2_s, Wl2_v, Wa):
        import jax, jax.numpy as jnp
        import numpy as np
        N = 2500
        E = 40000
        MUL0 = 64
        MUL1 = 32
        FC_IN = 16
        FC_H = 64
        WNUM = 192
        n = x.shape[0]
        x0 = x[:, :MUL0]
        x1 = x[:, MUL0:].reshape(n, MUL1, 3)
        a = node_attr
        h = jax.nn.silu(edge_scalars @ (Wfc1 / jnp.sqrt(jnp.float32(FC_IN))))
        w = h @ (Wfc2 / jnp.sqrt(jnp.float32(FC_H)))
        w0 = w[:, :64]
        w1 = w[:, 64:128]
        w2 = w[:, 128:160]
        w3 = w[:, 160:192]
        inv8 = 1.0 / jnp.sqrt(jnp.float32(MUL0))
        inv32 = 1.0 / jnp.sqrt(jnp.float32(MUL1))
        sc = jnp.concatenate([x0 @ Wsc0 * a * inv8, (jnp.einsum('num,uv->nvm', x1, Wsc1) * a[..., None] * inv32).reshape(n, 3 * MUL1)], axis=1)
        f0 = x0 @ Wl1_0 * a * inv8
        f1 = jnp.einsum('num,uv->nvm', x1, Wl1_1) * a[..., None] * inv32
        e0 = f0[edge_src]
        e1 = f1[edge_src]
        sh0 = edge_attr_sh[:, :1]
        sh1 = edge_attr_sh[:, 1:4]
        mid0 = w0 * e0 * sh0
        mid1 = w3 * jnp.einsum('eum,em->eu', e1, sh1) / jnp.sqrt(3.0)
        mid2 = w1[:, :, None] * e0[:, :, None] * sh1[:, None, :]
        mid3 = w2[:, :, None] * e1 * sh0[:, :, None]
        cnt = jnp.clip(jax.ops.segment_sum(jnp.ones(edge_dst.shape, x.dtype), edge_dst, num_segments=n), 1.0)

        def smean(v):
            s = jax.ops.segment_sum(v, edge_dst, num_segments=n)
            return s / cnt.reshape((n,) + (1,) * (v.ndim - 1))
        n0, n1 = (smean(mid0), smean(mid1))
        n2, n3 = (smean(mid2), smean(mid3))
        scal = jnp.concatenate([n0, n1], axis=1)
        vec = jnp.concatenate([n2, n3], axis=1)
        inv96 = 1.0 / jnp.sqrt(jnp.float32(MUL0 + MUL1))
        alpha = scal @ Wa * a * inv96
        out_s = scal @ Wl2_s * a * inv96
        out_v = jnp.einsum('num,uv->nvm', vec, Wl2_v) * a[..., None] * inv96
        conv = jnp.concatenate([out_s, out_v.reshape(n, 3 * MUL1)], axis=1)
        return sc + alpha * conv
    edge_index = jnp.stack([src, dst])
    x = _layernorm(x + _L0_gnn_ref(x, edge_index, edge_attr_4, edge_attr_16, L0_gnn_W_ss, L0_gnn_W_sv, L0_gnn_W_vs, L0_gnn_W_vv, L0_gnn_W_rad, L0_gnn_b_rad, L0_gnn_L_s, L0_gnn_L_v), axis=-1)
    x = _layernorm(x + _L1_gnn_ref(x, node_vec1, edge_attr_16, edge_attr_4, src, dst, L1_gnn_Wfc1, L1_gnn_Wfc2, L1_gnn_Wsc0, L1_gnn_Wsc1, L1_gnn_Wl1_0, L1_gnn_Wl1_1, L1_gnn_Wl2_s, L1_gnn_Wl2_v, L1_gnn_Wa), axis=-1)
    return x

_drawn_inputs = setup_inputs


def setup_inputs(seed=0):
    import zlib

    import numpy as np

    out = dict(_drawn_inputs(seed))
    spreads = {}
    factors = {'L1_gnn_Wfc1': 8.0,
     'L1_gnn_Wfc2': 8.0,
     'L1_gnn_Wl1_0': 8.0,
     'L1_gnn_Wl1_1': 8.0,
     'L1_gnn_Wl2_s': 8.0,
     'L1_gnn_Wl2_v': 8.0,
     'L1_gnn_Wa': 8.0,
     'L1_gnn_Wsc0': 6.452,
     'L1_gnn_Wsc1': 7.747}
    for name, (base, spread) in spreads.items():
        noise = np.random.default_rng([zlib.crc32(name.encode()), seed]).standard_normal(out[name].shape)
        drawn = base * np.exp(spread * noise) if base else spread * noise
        out[name] = jnp.asarray(drawn.astype(out[name].dtype))
    for name, factor in factors.items():
        out[name] = (out[name] * factor).astype(out[name].dtype)
    return out
```

```python
import concourse.bass as bass
from concourse import mybir
from contextlib import ExitStack

NODES, EDGES = 6250, 206250
MS, MV = 64, 32
DIM = MS + 3 * MV

P = 128
TPS = 4
SUP_EDGES = TPS * P
SLOTS = 4
SUPS = -(-EDGES // (SUP_EDGES * SLOTS)) * SLOTS
ROUNDS = SUPS // SLOTS
EDGES_PAD = SUPS * SUP_EDGES

GROUP = 7
NODE_TILES = -(-NODES // P)
GROUPS = NODE_TILES // GROUP
NODES_PAD = NODE_TILES * P
WIN = 32
WINDOWS = NODES_PAD // WIN
assert GROUPS * GROUP == NODE_TILES

FIN = 16
HID = 64
ROW0 = 384
ROW1 = DIM
MSG0 = 576
MSG1 = 320
REG0, REG1 = 3, 5
PAIR0 = 1
EPS = 1e-5
BANK = 512


def mk_gnn_resnorm_d2_gnn_r8_694f30_kernel(nc, a):
    f32, bf16, i32, i16 = mybir.dt.float32, mybir.dt.bfloat16, mybir.dt.int32, mybir.dt.int16
    ALU = mybir.AluOpType
    ACT = mybir.ActivationFunctionType
    AX = mybir.AxisListType
    ctx = ExitStack()
    with ctx:
        def sb(name, shape, dt=f32):
            return ctx.enter_context(nc.sbuf_tensor(name, shape, dt))

        def sem(name):
            return ctx.enter_context(nc.semaphore(name))

        arena = sb("arena", [P, REG1 * NODES_PAD])
        acc0 = arena[:, 0:REG0 * NODES_PAD].rearrange("p (r n) -> p r n", r=REG0)
        at = REG0 * NODES_PAD
        rows0 = arena[:, at:at + SLOTS * TPS * ROW0].rearrange("p (s t c) -> p s t c", s=SLOTS, t=TPS)
        at += SLOTS * TPS * ROW0
        msg0 = arena[:, at:at + 2 * TPS * MSG0].rearrange("p (s t c) -> p s t c", s=2, t=TPS)
        xt1 = arena[:, at:at + GROUP * 2 * P].rearrange("p (g h n) -> p g h n", g=GROUP, h=2)
        feat = arena[:, at + GROUP * 2 * P:at + GROUP * (2 * P + 2 * DIM)].rearrange("p (g c) -> p g c", g=GROUP)
        acc1 = arena[:, :].rearrange("p (r n) -> p r n", r=REG1)
        small = sb("small", [P, (SLOTS * ROW1 + 2 * MSG1) * TPS])
        rows1 = small[:, 0:SLOTS * TPS * ROW1].rearrange("p (s t c) -> p s t c", s=SLOTS, t=TPS)
        msg1 = small[:, SLOTS * TPS * ROW1:].rearrange("p (s t c) -> p s t c", s=2, t=TPS)
        xstage = small[:, 0:GROUP * 2 * P].rearrange("p (g h n) -> p g h n", g=GROUP, h=2)
        trows = small[:, GROUP * 2 * P:GROUP * (2 * P + ROW0)].rearrange("p (g c) -> p g c", g=GROUP)
        stage0 = small[:, 0:GROUP * REG0 * P].rearrange("p (g r n) -> p g r n", g=GROUP, r=REG0)
        stage1 = small[:, 0:GROUP * REG1 * P].rearrange("p (g r n) -> p g r n", g=GROUP, r=REG1)

        iota = sb("iota", [P, NODES_PAD], i16)
        srcs = sb("srcs", [P, SLOTS, TPS], i32)
        dst_sh = sb("dst_sh", [P, SLOTS, 5 * TPS], i32)
        escal = sb("escal", [FIN + 1, SLOTS, SUP_EDGES])
        hid = sb("hid", [HID, 2, SUP_EDGES])
        onehot = sb("onehot", [P, 2 * TPS * WIN], bf16)
        sel = sb("sel", [P, 2 * TPS * 4 * WIN])
        ones = sb("ones", [P, P], bf16)
        one = sb("one", [1, 1])
        zeros = sb("zeros", [P, REG1 * WIN])
        ident = sb("ident", [P, P])
        attr = sb("attr", [P, NODE_TILES])
        gain = sb("gain", [P, NODE_TILES])
        group = sb("group", [P, 4, GROUP, DIM])
        xg, tg, sq, og = (group[:, k] for k in range(4))
        stat = sb("stat", [P, 8, GROUP])
        wtab = sb("wtab", [1, 3, SUPS], i32)
        wtabf = group[0:1, :, :, :].rearrange("p k g c -> p (k g c)")[:, 0:4 * SUPS].rearrange("p (k s) -> p k s", k=4)
        wends = sb("wends", [ROUNDS, 2, SLOTS])
        dsts = arena[0:ROUNDS, REG0 * NODES_PAD:REG0 * NODES_PAD + SLOTS * SUP_EDGES].bitcast(i32).rearrange(
            "p (s e) -> p s e", s=SLOTS)
        w0a, w0b = sb("w0a", [P, 3 * 96]), sb("w0b", [MV, 96])
        la, lb = sb("la", [P, DIM]), sb("lb", [96, DIM])
        wfa, wfb = sb("wfa", [P, 2 * P]), sb("wfb", [MV, 2 * MV])
        wrad = sb("wrad", [FIN + 1, DIM])
        fc1, fc2 = sb("fc1", [FIN, HID]), sb("fc2", [HID, 192])
        wout = sb("wout", [P, REG1, DIM + 1])

        ps = ctx.enter_context(nc.psum_tensor("ps", [P, 8 * BANK], f32))

        def bank(b, n=1):
            return ps[:, b * BANK:(b + n) * BANK]

        def two_to_a_bank(b, n):
            return bank(b, 2).rearrange("p (t c) -> p t c", t=TPS)[:, :, 0:n]

        rad = [two_to_a_bank(2 * b, DIM) for b in range(2)]
        wps = [two_to_a_bank(2 * b, 192) for b in range(2)]
        hps = [bank(4 + b) for b in range(2)]
        AGG = 6
        yps = bank(0, 4).rearrange("p (g c) -> p g c", c=BANK // 2)
        tps_, fps = [bank(4), bank(5)], [bank(6), bank(7)]

        def dram(name, shape):
            return nc.dram_tensor(name, shape, f32, kind="Internal").ap()

        table0, table1 = dram("table0", [NODES_PAD, ROW0]), dram("table1", [NODES_PAD, ROW1])
        base_d, wends_d = dram("base_d", [NODES_PAD, DIM]), dram("wends_d", [2, SUPS])

        def node_rows(t, g):
            return t[bass.ds(g * (GROUP * P), GROUP * P), :].rearrange("(g p) c -> p g c", p=P)

        s_weights, s_wscaled = sem("weights_loaded"), sem("weights_scaled")
        s_const = sem("constants_made")
        s_dsts, s_ends, s_endsout, s_endsin = sem("dsts_loaded"), sem("ends_found"), sem("ends_stored"), sem("ends_loaded")
        s_wstep, s_wtab = sem("window_step"), sem("window_table_made")
        s_zero0, s_zero1, s_acc0x = sem("sums0_zeroed"), sem("sums1_zeroed"), sem("sums0_have_x")
        s_xst = [sem(f"x_tile_loaded{j}") for j in range(GROUP)]
        s_tmm, s_tev, s_tst = sem("table0_product"), [sem("table0_by_act"), sem("table0_by_dve")], [sem(f"table0_stored{j}") for j in range(GROUP)]
        s_src = [[sem(f"srcs_loaded{l}_{j}") for j in range(SLOTS)] for l in range(2)]
        s_dsh = [[sem(f"dst_sh_loaded{l}_{j}") for j in range(SLOTS)] for l in range(2)]
        s_esc = [[sem(f"edge_scalars_loaded{l}_{j}") for j in range(SLOTS)] for l in range(2)]
        s_rows = [[sem(f"rows_gathered{l}_{j}") for j in range(SLOTS)] for l in range(2)]
        s_pool = sem("pool_went_on")
        s_lin, s_act = [sem(f"radial_product{l}") for l in range(2)], [sem(f"radial_activated{l}") for l in range(2)]
        s_w2 = sem("radial_weights")
        s_msg = [sem(f"messages_made{l}") for l in range(2)]
        s_oh, s_sel = [sem(f"onehot_made{l}") for l in range(2)], [sem(f"selection_made{l}") for l in range(2)]
        s_agg, s_flush = [sem(f"pair_summed{l}") for l in range(2)], [sem(f"pair_added{l}") for l in range(2)]
        s_done = [sem(f"sums_complete{l}") for l in range(2)]
        s_xin, s_xin1 = sem("x_rows_loaded"), sem("base_rows_loaded")
        s_stage, s_y = [sem(f"sums_staged{l}") for l in range(2)], [sem(f"node_product{l}") for l in range(2)]
        s_ln, s_lnact = [sem(f"norm_step{l}") for l in range(2)], [sem(f"norm_act{l}") for l in range(2)]
        s_tp, s_tpe, s_f, s_fev = sem("x1_transposed"), sem("x1t_copied"), sem("features"), sem("features_copied")
        s_base, s_fst, s_out = sem("base_ready"), sem("table1_stored"), sem("out_stored")

        WEIGHTS = [(w0a, "w0a"), (w0b, "w0b"), (la, "la"), (lb, "lb"), (wfa, "wfa"), (wfb, "wfb"),
                   (wrad, "wrad"), (fc1, "fc1"), (fc2, "fc2"), (wout, "wout"), (attr, "attr")]
        ISQ3, ISQ2 = 3.0 ** -0.5, 2.0 ** -0.5
        I8, I32, I96 = MS ** -0.5, MV ** -0.5, (MS + MV) ** -0.5
        SCALED = [(w0a[0:64, 0:64], I8 * ISQ2), (w0a[0:64, 64:96], I8 * ISQ3 * ISQ2),
                  (w0a[64:128, 96:288], I32 * ISQ3 * ISQ2), (w0b[:], I32 * ISQ3 * ISQ2),
                  (la[0:64, :], I8), (la[64:128, :], I32), (lb[0:64, :], I8), (lb[64:96, :], I32),
                  (wfa[0:64, :], I8), (wfa[64:128, :], I32), (wfb[:], I32),
                  (fc1[:], FIN ** -0.5), (fc2[:], HID ** -0.5),
                  (wout[:, 0, :], I96), (wout[0:64, 1, :], I96), (wout[64:96, 1, :], I96 * ISQ3),
                  (wout[96:128, 1, :], I96), (wout[0:96, 2, :], I96), (wout[96:128, 2, :], I96 * ISQ3),
                  (wout[0:32, 3, :], I96), (wout[32:64, 3, :], I96 * ISQ3), (wout[64:128, 3, :], I96),
                  (wout[:, 4, :], I96)]
        LN_STEPS = [12, 11]
        block = ctx.enter_context(nc.Block())

        @block.sync
        def _(sp):
            sp.dma_start(dsts, a["dsts"]).then_inc(s_dsts, 16)
            for t, name in WEIGHTS:
                sp.dma_start(t[:], a[name]).then_inc(s_weights, 16)

            def load_x(g, j):
                at = g * (GROUP * P) + j * P
                sp.dma_start(xstage[:, j, 0, :], a["xT"][0:P, bass.ds(at, P)]).then_inc(s_xst[j], 16)
                sp.dma_start(xstage[0:MV, j, 1, :], a["xT"][P:DIM, bass.ds(at, P)]).then_inc(s_xst[j], 16)

            for j in range(GROUP):
                load_x(0, j)
            sp.wait_ge(s_ends, 2)
            for e in range(2):
                sp.dma_start(wends_d[e:e + 1, :].rearrange("o (p s) -> (o p) s", s=SLOTS),
                             wends[:, e, :]).then_inc(s_endsout, 16)
            sp.wait_ge(s_endsout, 32)
            sp.dma_start(wtabf[:, 0:2, :], wends_d.rearrange("(o e) s -> o e s", o=1)).then_inc(s_endsin, 16)

            def store_row(g, j):
                by, of = j % 2, (GROUP + 1 - j % 2) // 2
                sp.wait_ge(s_tev[by], g * of + j // 2 + 1)
                at = g * (GROUP * P) + j * P
                sp.dma_start(table0[bass.ds(at, P), :], trows[:, j, :]).then_inc(s_tst[j], 16)

            with sp.Fori(0, GROUPS - 1) as g:
                for j in range(GROUP):
                    store_row(g, j)
                    load_x(g + 1, j)
            for j in range(GROUP):
                store_row(GROUPS - 1, j)
            sp.wait_ge(s_zero0, 3)
            sp.dma_start(acc0[:, 0, :], a["xT"][0:P, :]).then_inc(s_acc0x, 16)
            sp.dma_start(acc0[64:96, 1, :], a["xT"][P:DIM, :]).then_inc(s_acc0x, 16)

            def load_src(l, s, j):
                sp.dma_start(srcs[:, j, :], a["srcs"][bass.ds(s, 1), :, :].rearrange("o p c -> (o p) c")).then_inc(s_src[l][j], 16)

            def load_dst_sh(l, s, j):
                sp.dma_start(dst_sh[:, j, :], a["dst_sh"][bass.ds(s, 1), :, :].rearrange("o p c -> (o p) c")).then_inc(s_dsh[l][j], 16)

            def load_escal(l, s, j):
                sp.dma_start(escal[0:FIN, j, :], a["escal"][:, bass.ds(s * SUP_EDGES, SUP_EDGES)]).then_inc(s_esc[l][j], 16)

            for l in range(2):
                if l == 0:
                    sp.wait_ge(s_const, 5)
                else:
                    sp.wait_ge(s_done[0], 1)
                for j in range(SLOTS):
                    load_src(l, j, j)
                    load_escal(l, j, j)
                    load_dst_sh(l, j, j)
                with sp.Fori(0, ROUNDS - 1) as i:
                    for j in range(SLOTS):
                        s = i * SLOTS + j
                        sp.wait_ge(s_rows[l][j], (i + 1) * 16 * TPS)
                        load_src(l, s + SLOTS, j)
                        sp.wait_ge(s_lin[l], s + 1)
                        load_escal(l, s + SLOTS, j)
                        sp.wait_ge(s_msg[l], s + 2)
                        load_dst_sh(l, s + SLOTS, j)
                if l == 0:
                    sp.dma_start(xg, node_rows(a["xd"], 0)).then_inc(s_xin, 16)
                    def store_features(g):
                        sp.wait_ge(s_base, g + 1)
                        sp.dma_start(node_rows(table1, g), feat[:, :, 0:DIM]).then_inc(s_fst, 16)
                        sp.dma_start(node_rows(base_d, g), feat[:, :, DIM:2 * DIM]).then_inc(s_fst, 16)

                    with sp.Fori(0, GROUPS - 1) as g:
                        sp.wait_ge(s_ln[0], g * LN_STEPS[0] + 1)
                        sp.dma_start(xg, node_rows(a["xd"], g + 1)).then_inc(s_xin, 16)
                        store_features(g)
                    store_features(GROUPS - 1)

            sp.wait_ge(s_fst, 32 * GROUPS)
            sp.wait_ge(s_ln[0], GROUPS * LN_STEPS[0])
            sp.dma_start(xg, node_rows(base_d, 0)).then_inc(s_xin1, 16)

            def store_out(g):
                sp.wait_ge(s_ln[1], (g + 1) * LN_STEPS[1])
                sp.dma_start(node_rows(a["out"], g), og).then_inc(s_out, 16)

            with sp.Fori(0, GROUPS - 1) as g:
                sp.wait_ge(s_ln[1], g * LN_STEPS[1] + 3)
                sp.dma_start(xg, node_rows(base_d, g + 1)).then_inc(s_xin1, 16)
                store_out(g)
            store_out(GROUPS - 1)
            sp.wait_ge(s_out, 16 * GROUPS)

        @block.gpsimd
        def _(pool):
            nc.gpsimd.memset(zeros[:], 0.0).then_inc(s_const, 1)
            nc.gpsimd.memset(ones[:], 1.0).then_inc(s_const, 1)
            nc.gpsimd.memset(one[:], 1.0).then_inc(s_const, 1)
            nc.gpsimd.memset(ident[:], 0.0).then_inc(s_const, 1)
            nc.gpsimd.memset(escal[:], 1.0).then_inc(s_const, 1)
            pool.wait_ge(s_const, 4)
            nc.gpsimd.affine_select(out=ident[:], in_=ident[:], compare_op=ALU.not_equal, fill=1.0, base=0,
                                    pattern=[[-1, P]], channel_multiplier=1).then_inc(s_const, 1)
            nc.gpsimd.iota(iota[:], pattern=[[1, NODES_PAD]], base=0, channel_multiplier=0).then_inc(s_const, 1)
            pool.wait_ge(s_ends, 2)
            nc.gpsimd.memset(msg0, 0.0).then_inc(s_zero0, 1)
            nc.gpsimd.memset(acc0[:, 1, :], 0.0).then_inc(s_zero0, 1)
            nc.gpsimd.memset(acc0[:, 2, :], 0.0).then_inc(s_zero0, 1)

            def gather(l, j):
                rows, table = (rows0, table0) if l == 0 else (rows1, table1)
                for t in range(TPS):
                    pool.indirect_dma_start(
                        out=rows[:, j, t, :], out_offset=None, in_=table,
                        in_offset=bass.IndirectOffsetOnAxis(ap=srcs[:, j, t:t + 1], axis=0)).then_inc(s_rows[l][j], 16)

            def gathers(l):
                for j in range(SLOTS):
                    pool.wait_ge(s_src[l][j], 16)
                    gather(l, j)
                if l == 1:
                    nc.gpsimd.memset(arena[:, REG1 * NODES_PAD // 2:], 0.0).then_inc(s_zero1, 1)
                with pool.Fori(0, ROUNDS - 1) as i:
                    for j in range(SLOTS):
                        s = i * SLOTS + j
                        pool.wait_ge(s_msg[l], s + 1)
                        pool.sem_inc(s_pool, 1)
                        pool.wait_ge(s_src[l][j], (i + 2) * 16)
                        pool.sem_inc(s_pool, 1)
                        gather(l, j)

            def stage(l, g, j, first):
                if not first:
                    pool.wait_ge(s_y[l], (g - 1) * GROUP + j + 1)
                acc, to = (acc0, stage0) if l == 0 else (acc1, stage1)
                nc.gpsimd.tensor_copy(to[:, j, :, :], acc[:, :, bass.ds(g * (GROUP * P) + j * P, P)]).then_inc(s_stage[l], 1)

            for j in range(GROUP):
                pool.wait_ge(s_tst[j], 16 * GROUPS)
            gathers(0)

            pool.wait_ge(s_done[0], 1)
            for j in range(GROUP):
                stage(0, 0, j, True)

            def base(g):
                pool.wait_ge(s_fev, (g + 1) * GROUP)
                pool.wait_ge(s_ln[0], (g + 1) * LN_STEPS[0])
                nc.gpsimd.tensor_tensor(feat[:, :, DIM:2 * DIM], feat[:, :, DIM:2 * DIM], og, ALU.add).then_inc(s_base, 1)

            with pool.Fori(0, GROUPS - 1) as g:
                for j in range(GROUP):
                    stage(0, g + 1, j, False)
                base(g)
            base(GROUPS - 1)

            pool.wait_ge(s_fst, 32 * GROUPS)
            gathers(1)
            pool.wait_ge(s_done[1], 1)
            for j in range(GROUP):
                stage(1, 0, j, True)
            with pool.Fori(1, GROUPS) as g:
                for j in range(GROUP):
                    stage(1, g, j, False)

        @block.scalar
        def _(act):
            def table_row(g, j, first):
                act.wait_ge(s_tmm, g * GROUP + j + 1)
                if not first:
                    act.wait_ge(s_tst[j], g * 16)
                p, r = bank(j), trows[:, j, :]
                nc.scalar.activation(r[:, 32:96], p[:, 0:64], ACT.Copy)
                nc.scalar.activation(r[:, 352:384], p[:, 64:96], ACT.Copy)
                nc.scalar.activation(r[:, 160:352].rearrange("p (d c) -> p d c", d=3),
                                     p[:, 96:384].rearrange("p (d c) -> p d c", d=3)[:, :, 0:64], ACT.Copy)
                nc.scalar.activation(r[:, 96:160].rearrange("p (d c) -> p d c", d=2),
                                     p[:, 160:352].rearrange("p (d c) -> p d c", d=2)[:, :, 0:32], ACT.Copy)
                nc.scalar.activation(r[:, 0:32], p[:, 352:384], ACT.Copy).then_inc(s_tev[0], 1)

            for j in range(0, GROUP, 2):
                table_row(0, j, True)
            with act.Fori(1, GROUPS) as g:
                for j in range(0, GROUP, 2):
                    table_row(g, j, False)

            def sigmoid(s, j):
                act.wait_ge(s_lin[0], s + 1)
                nc.scalar.activation(rad[j % 2], rad[j % 2], ACT.Sigmoid).then_inc(s_act[0], 1)

            with act.Fori(0, ROUNDS) as i:
                for j in range(SLOTS):
                    sigmoid(i * SLOTS + j, j)

            def norm_act(l, g, square_at, sqrt_at):
                act.wait_ge(s_ln[l], g * LN_STEPS[l] + square_at)
                nc.scalar.activation(sq, tg, ACT.Square).then_inc(s_lnact[l], 1)
                act.wait_ge(s_ln[l], g * LN_STEPS[l] + sqrt_at)
                nc.scalar.activation(stat[:, 6, :], stat[:, 5, :], ACT.Sqrt).then_inc(s_lnact[l], 1)

            def features(g, first):
                if not first:
                    act.wait_ge(s_fst, g * 32)
                for j in range(GROUP):
                    n = g * GROUP + j
                    act.wait_ge(s_tp, n + 1)
                    nc.scalar.activation(xt1[:, j, 0, :], tps_[j % 2][:, 0:P], ACT.Copy)
                    nc.scalar.activation(xt1[0:MV, j, 1, :], tps_[j % 2][0:MV, P:2 * P], ACT.Copy).then_inc(s_tpe, 1)
                    act.wait_ge(s_f, n + 1)
                    nc.scalar.activation(feat[:, j, :], fps[j % 2][:, 0:2 * DIM], ACT.Copy,
                                         scale=attr[:, bass.ds(n, 1)]).then_inc(s_fev, 1)

            act.wait_ge(s_done[0], 1)
            norm_act(0, 0, 8, 10)
            features(0, True)
            with act.Fori(1, GROUPS) as g:
                norm_act(0, g, 8, 10)
                features(g, False)

            def silu(s, j):
                act.wait_ge(s_lin[1], s + 1)
                nc.scalar.activation(hid[:, j % 2, :], hps[j % 2][0:HID, :], ACT.Silu).then_inc(s_act[1], 1)

            with act.Fori(0, ROUNDS) as i:
                for j in range(SLOTS):
                    silu(i * SLOTS + j, j)

            with act.Fori(0, GROUPS) as g:
                norm_act(1, g, 6, 8)

        @block.vector
        def _(dve):
            dve.wait_ge(s_dsts, 16)
            nc.vector.tensor_reduce(wends[:, 0, :], dsts, AX.X, ALU.min).then_inc(s_ends, 1)
            nc.vector.tensor_reduce(wends[:, 1, :], dsts, AX.X, ALU.max).then_inc(s_ends, 1)
            dve.wait_ge(s_weights, 16 * len(WEIGHTS))
            for w, c in SCALED:
                nc.vector.tensor_scalar(w, w, c, None, ALU.mult).then_inc(s_wscaled, 1)
            dve.wait_ge(s_endsin, 16)
            nc.vector.tensor_copy(wtab[:, 0:2, :], wtabf[:, 0:2, :]).then_inc(s_wstep, 1)
            dve.wait_ge(s_wstep, 1)
            nc.vector.tensor_scalar(wtab[:, 0:2, :], wtab[:, 0:2, :], WIN.bit_length() - 1, None,
                                    ALU.arith_shift_right).then_inc(s_wstep, 1)
            dve.wait_ge(s_wstep, 2)
            nc.vector.tensor_copy(wtabf[:, 0:2, :], wtab[:, 0:2, :]).then_inc(s_wstep, 1)
            dve.wait_ge(s_wstep, 3)
            nc.vector.scalar_tensor_tensor(wtabf[:, 1, :], wtabf[:, 1, :], 1.0, wtabf[:, 0, :],
                                           ALU.add, ALU.subtract).then_inc(s_wstep, 1)
            dve.wait_ge(s_wstep, 4)
            nc.vector.tensor_tensor_scan(wtabf[:, 2, :], wtabf[:, 1, :], wtabf[:, 1, :], float(PAIR0),
                                         ALU.add, ALU.bypass).then_inc(s_wstep, 1)
            dve.wait_ge(s_wstep, 5)
            nc.vector.tensor_tensor(wtabf[:, 3, :], wtabf[:, 2, :], wtabf[:, 1, :], ALU.subtract).then_inc(s_wstep, 1)
            dve.wait_ge(s_wstep, 6)
            nc.vector.tensor_copy(wtab[:, 1, :], wtabf[:, 1, :]).then_inc(s_wtab, 1)
            nc.vector.tensor_copy(wtab[:, 2, :], wtabf[:, 3, :]).then_inc(s_wtab, 1)

            def table_row(g, j, first):
                dve.wait_ge(s_tmm, g * GROUP + j + 1)
                if not first:
                    dve.wait_ge(s_tst[j], g * 16)
                p, r = bank(j), trows[:, j, :]
                nc.vector.tensor_copy(r[:, 32:96], p[:, 0:64])
                nc.vector.tensor_copy(r[:, 352:384], p[:, 64:96])
                nc.vector.tensor_copy(r[:, 160:352].rearrange("p (d c) -> p d c", d=3),
                                      p[:, 96:384].rearrange("p (d c) -> p d c", d=3)[:, :, 0:64])
                nc.vector.tensor_copy(r[:, 96:160].rearrange("p (d c) -> p d c", d=2),
                                      p[:, 160:352].rearrange("p (d c) -> p d c", d=2)[:, :, 0:32])
                nc.vector.tensor_copy(r[:, 0:32], p[:, 352:384]).then_inc(s_tev[1], 1)

            for j in range(1, GROUP, 2):
                table_row(0, j, True)
            with dve.Fori(1, GROUPS) as g:
                for j in range(1, GROUP, 2):
                    table_row(g, j, False)

            def bc(x, axis, shape):
                return x.unsqueeze(axis).to_broadcast(shape)

            def messages0(j):
                r, m, c = rows0[:, j, :, :], msg0[:, j % 2, :, :], rad[j % 2]
                nc.vector.tensor_tensor(m[:, :, 64:224], r[:, :, 0:160], c, ALU.mult)
                nc.vector.tensor_tensor(
                    m[:, :, 192:576].rearrange("p t (d c) -> p t d c", d=3)[:, :, :, 32:96],
                    r[:, :, 160:352].rearrange("p t (d c) -> p t d c", d=3),
                    bc(c[:, :, 32:96], 2, [P, TPS, 3, MS]), ALU.mult)
                nc.vector.tensor_tensor(
                    m[:, :, 256:576].rearrange("p t (d c) -> p t d c", d=2)[:, :, :, 32:64],
                    bc(r[:, :, 352:384], 2, [P, TPS, 2, MV]),
                    c[:, :, 96:160].rearrange("p t (d c) -> p t d c", d=2), ALU.mult)
                nc.vector.tensor_tensor(m[:, :, 544:576], r[:, :, 352:384], c[:, :, 0:32],
                                        ALU.mult).then_inc(s_msg[0], 1)

            def messages1(j):
                r, m, w = rows1[:, j, :, :], msg1[:, j % 2, :, :], wps[j % 2]

                def two(x):
                    return x.rearrange("p t (k c) -> p t k c", k=2)

                nc.vector.tensor_tensor(two(m[:, :, 0:64]), bc(r[:, :, 0:32], 2, [P, TPS, 2, MV]), two(w[:, :, 0:64]), ALU.mult)
                nc.vector.tensor_tensor(two(m[:, :, 64:320])[:, :, :, 0:64], bc(r[:, :, 32:96], 2, [P, TPS, 2, MS]),
                                        two(w[:, :, 64:192]), ALU.mult)
                nc.vector.tensor_tensor(two(m[:, :, 128:192]), two(r[:, :, 96:160]),
                                        bc(w[:, :, 32:64], 2, [P, TPS, 2, MV]), ALU.mult)
                nc.vector.tensor_tensor(two(m[:, :, 256:320]), two(r[:, :, 96:160]),
                                        bc(w[:, :, 0:32], 2, [P, TPS, 2, MV]), ALU.mult).then_inc(s_msg[1], 1)

            def add_pair_before(l, pair, node):
                acc, regs = (acc0, REG0) if l == 0 else (acc1, REG1)
                dve.wait_ge(s_agg[l], pair)
                dve.wait_ge(s_flush[l], pair)
                to = acc[:, :, bass.ds(node, WIN)]
                nc.vector.tensor_tensor(
                    to, to, ps[:, bass.ds(((pair + 1) % 2) * BANK + AGG * BANK, regs * WIN)].rearrange("p (r w) -> p r w", r=regs),
                    ALU.add).then_inc(s_flush[l], 1)

            def windows(l, s, j, before):
                first = dve.value_load(wtab[0:1, 0, bass.ds(s, 1)], min_val=0, max_val=WINDOWS - 1)
                count = dve.value_load(wtab[0:1, 1, bass.ds(s, 1)], min_val=1, max_val=WINDOWS)
                pair0 = dve.value_load(wtab[0:1, 2, bass.ds(s, 1)], min_val=PAIR0, max_val=PAIR0 + SUPS * WINDOWS)
                with dve.Fori(0, count) as k:
                    pair = dve.snap(pair0 + k)
                    node = dve.snap(first + k).with_bounds(min_val=0, max_val=WINDOWS - 1) * WIN
                    oh = onehot[:, bass.ds((pair % 2) * (TPS * WIN), TPS * WIN)].rearrange("p (t w) -> p t w", t=TPS)
                    nc.vector.tensor_tensor(oh, bc(iota[:, bass.ds(node, WIN)], 1, [P, TPS, WIN]),
                                            bc(dst_sh[:, j, 0:TPS], 2, [P, TPS, WIN]), ALU.is_equal).then_inc(s_oh[l], 1)
                    dve.wait_ge(s_oh[l], pair)
                    nc.vector.tensor_tensor(
                        sel[:, bass.ds((pair % 2) * (4 * TPS * WIN), 4 * TPS * WIN)].rearrange("p (t k w) -> p t k w", t=TPS, k=4),
                        bc(oh, 2, [P, TPS, 4, WIN]),
                        bc(dst_sh[:, j, TPS:5 * TPS].bitcast(f32).rearrange("p (t k) -> p t k", t=TPS), 3, [P, TPS, 4, WIN]),
                        ALU.mult).then_inc(s_sel[l], 1)
                    add_pair_before(l, pair, dve.snap(before, min_val=0, max_val=NODES_PAD - WIN))
                    dve.reg_mov(before, node)

            def edge_layer(l):
                before = dve.alloc_register(f"window_before{l}")
                dve.reg_mov(before, 0)
                dve.sem_inc(s_flush[l], 1)

                def supertile(s, i, j):
                    dve.wait_ge(s_rows[l][j], (i + 1) * 16 * TPS)
                    dve.wait_ge(s_act[l], s + 1)
                    if l == 0:
                        messages0(j)
                    else:
                        dve.wait_ge(s_w2, s + 1)
                        messages1(j)
                    dve.wait_ge(s_dsh[l][j], (i + 1) * 16)
                    windows(l, s, j, before)

                with dve.Fori(0, ROUNDS) as i:
                    for j in range(SLOTS):
                        supertile(i * SLOTS + j, i, j)
                last = dve.value_load(wtab[0:1, 2, SUPS - 1:SUPS], min_val=PAIR0, max_val=PAIR0 + SUPS * WINDOWS)
                count = dve.value_load(wtab[0:1, 1, SUPS - 1:SUPS], min_val=1, max_val=WINDOWS)
                pairs = dve.snap(last + count)
                add_pair_before(l, pairs, dve.snap(before, min_val=0, max_val=NODES_PAD - WIN))
                dve.wait_ge(s_flush[l], pairs + 1)
                dve.sem_inc(s_done[l], 1)

            dve.wait_ge(s_const, 6)
            dve.wait_ge(s_acc0x, 32)
            dve.wait_ge(s_wtab, 2)
            edge_layer(0)

            def norm(l, g, n):
                base = g * LN_STEPS[l] + n
                dve.wait_ge(s_ln[l], base)
                nc.vector.tensor_reduce(stat[:, 3, :], tg, AX.X, ALU.add, negate=True).then_inc(s_ln[l], 1)
                dve.wait_ge(s_ln[l], base + 1)
                nc.vector.tensor_scalar(stat[:, 4, :], stat[:, 3, :], 1.0 / DIM, None, ALU.mult).then_inc(s_ln[l], 1)
                dve.wait_ge(s_ln[l], base + 2)
                nc.vector.tensor_tensor(tg, tg, bc(stat[:, 4, :], 2, [P, GROUP, DIM]), ALU.add).then_inc(s_ln[l], 1)
                dve.wait_ge(s_lnact[l], g * 2 + 1)
                nc.vector.tensor_reduce(stat[:, 0, :], sq, AX.X, ALU.add).then_inc(s_ln[l], 1)
                dve.wait_ge(s_ln[l], base + 4)
                nc.vector.tensor_scalar(stat[:, 5, :], stat[:, 0, :], 1.0 / DIM, EPS, ALU.mult, ALU.add).then_inc(s_ln[l], 1)
                dve.wait_ge(s_lnact[l], g * 2 + 2)
                nc.vector.reciprocal(stat[:, 7, :], stat[:, 6, :]).then_inc(s_ln[l], 1)
                dve.wait_ge(s_ln[l], base + 6)

            def nodes0(g, first):
                base = g * LN_STEPS[0]
                dve.wait_ge(s_y[0], (g + 1) * GROUP)
                dve.wait_ge(s_xin, (g + 1) * 16)
                if not first:
                    dve.wait_ge(s_ln[0], base)
                nc.vector.tensor_tensor(tg, yps[:, 0:GROUP, 0:DIM], xg, ALU.add).then_inc(s_ln[0], 1)
                nc.vector.tensor_scalar(stat[:, 0, :], yps[:, 0:GROUP, DIM], 1.0, None, ALU.max).then_inc(s_ln[0], 1)
                dve.wait_ge(s_ln[0], base + 2)
                nc.vector.reciprocal(stat[:, 1, :], stat[:, 0, :]).then_inc(s_ln[0], 1)
                dve.wait_ge(s_ln[0], base + 3)
                nc.vector.tensor_tensor(stat[:, 2, :], stat[:, 1, :], attr[:, bass.ds(g * GROUP, GROUP)], ALU.mult).then_inc(s_ln[0], 1)
                dve.wait_ge(s_ln[0], base + 4)
                nc.vector.tensor_tensor(gain[:, bass.ds(g * GROUP, GROUP)], stat[:, 2, :], stat[:, 2, :], ALU.mult).then_inc(s_ln[0], 1)
                norm(0, g, 5)
                if not first:
                    dve.wait_ge(s_base, g)
                nc.vector.tensor_tensor(og, tg, bc(stat[:, 7, :], 2, [P, GROUP, DIM]), ALU.mult).then_inc(s_ln[0], 1)

            nodes0(0, True)
            with dve.Fori(1, GROUPS) as g:
                nodes0(g, False)

            dve.wait_ge(s_stage[0], GROUPS * GROUP)
            dve.wait_ge(s_fst, 32 * GROUPS)
            nc.vector.memset(arena[:, 0:REG1 * NODES_PAD // 2], 0.0).then_inc(s_zero1, 1)
            dve.wait_ge(s_zero1, 2)
            edge_layer(1)

            def nodes1(g, first):
                base = g * LN_STEPS[1]
                dve.wait_ge(s_y[1], (g + 1) * GROUP)
                if not first:
                    dve.wait_ge(s_ln[1], base)
                nc.vector.tensor_tensor(stat[:, 0, :], yps[:, 0:GROUP, DIM], gain[:, bass.ds(g * GROUP, GROUP)], ALU.mult).then_inc(s_ln[1], 1)
                dve.wait_ge(s_ln[1], base + 1)
                nc.vector.tensor_tensor(tg, yps[:, 0:GROUP, 0:DIM], bc(stat[:, 0, :], 2, [P, GROUP, DIM]), ALU.mult).then_inc(s_ln[1], 1)
                dve.wait_ge(s_xin1, (g + 1) * 16)
                dve.wait_ge(s_ln[1], base + 2)
                nc.vector.tensor_tensor(tg, tg, xg, ALU.add).then_inc(s_ln[1], 1)
                norm(1, g, 3)
                if not first:
                    dve.wait_ge(s_out, g * 16)
                nc.vector.tensor_tensor(og[:, :, 0:MS], tg[:, :, 0:MS], bc(stat[:, 7, :], 2, [P, GROUP, MS]), ALU.mult).then_inc(s_ln[1], 1)
                nc.vector.tensor_tensor(og[:, :, MS:DIM].rearrange("p g (v d) -> p g d v", d=3),
                                        tg[:, :, MS:DIM].rearrange("p g (d v) -> p g d v", d=3),
                                        bc(stat[:, 7, :].unsqueeze(2), 3, [P, GROUP, 3, MV]), ALU.mult).then_inc(s_ln[1], 1)

            nodes1(0, True)
            with dve.Fori(1, GROUPS) as g:
                nodes1(g, False)

        @block.tensor
        def _(pe):
            mm = nc.tensor.matmul
            pe.wait_ge(s_wscaled, len(SCALED))
            pe.wait_ge(s_const, 6)

            def table_product(g, j, first):
                pe.wait_ge(s_xst[j], (g + 1) * 32)
                if not first:
                    by, of = j % 2, (GROUP + 1 - j % 2) // 2
                    pe.wait_ge(s_tev[by], (g - 1) * of + j // 2 + 1)
                x, p = xstage[:, j, :, :], bank(j)
                mm(p[:, 0:288], x[:, 0, :], w0a[:], start=True, stop=True)
                mm(p[:, 288:384], x[0:32, 1, :], w0b[:], start=True, stop=True).then_inc(s_tmm, 1)

            for j in range(GROUP):
                table_product(0, j, True)
            with pe.Fori(1, GROUPS) as g:
                for j in range(GROUP):
                    table_product(g, j, False)
            pe.wait_ge(s_tev[0], GROUPS * ((GROUP + 1) // 2))
            pe.wait_ge(s_tev[1], GROUPS * (GROUP // 2))
            pe.wait_ge(s_wtab, 2)

            def radial0(s, i, j):
                pe.wait_ge(s_esc[0][j], (i + 1) * 16)
                for t in range(TPS):
                    last = mm(rad[j % 2][:, t, :], escal[:, j, t * P:(t + 1) * P], wrad[:], start=True, stop=True)
                last.then_inc(s_lin[0], 1)

            def hidden1(s, i, j):
                pe.wait_ge(s_esc[1][j], (i + 1) * 16)
                mm(hps[j % 2][0:HID, :], fc1[:], escal[0:FIN, j, :], start=True, stop=True).then_inc(s_lin[1], 1)

            def radial1(s, j):
                pe.wait_ge(s_act[1], s + 1)
                for t in range(TPS):
                    last = mm(wps[j % 2][:, t, :], hid[:, j % 2, t * P:(t + 1) * P], fc2[:], start=True, stop=True)
                last.then_inc(s_w2, 1)

            def sum_pair0(pair, j):
                def moving(t, k):
                    return sel[:, bass.ds((pair % 2) * (4 * TPS * WIN) + (t * 4 + k) * WIN, WIN)]

                def sums(r, rows=P):
                    return ps[0:rows, bass.ds((pair % 2) * BANK + AGG * BANK + r * WIN, WIN)]

                for t in range(TPS):
                    m, stop = msg0[:, j % 2, t, :], t == TPS - 1
                    mm(sums(0), m[:, 96:224], moving(t, 3), start=t == 0, stop=False, skip_group_check=True)
                    mm(sums(1), m[:, 0:128], moving(t, 3), start=False, stop=False, skip_group_check=True)
                    mm(sums(0, 96), m[:, 224:320], moving(t, 0), start=False, stop=False, skip_group_check=True)
                    mm(sums(0), m[:, 352:480], moving(t, 1), start=False, stop=stop, skip_group_check=True)
                    mm(sums(1, 96), m[:, 480:576], moving(t, 2), start=False, stop=stop, skip_group_check=True)
                    last = mm(sums(2), ones[:], onehot[:, bass.ds((pair % 2) * (TPS * WIN) + t * WIN, WIN)],
                              start=False, stop=stop, skip_group_check=True)
                last.then_inc(s_agg[0], 1)

            def sum_pair1(pair, j):
                def moving(t, k, n):
                    return sel[:, bass.ds((pair % 2) * (4 * TPS * WIN) + (t * 4 + k) * WIN, n * WIN)]

                def sums(r, n):
                    return ps[:, bass.ds((pair % 2) * BANK + AGG * BANK + r * WIN, n * WIN)]

                for t in range(TPS):
                    m, stop = msg1[:, j % 2, t, :], t == TPS - 1
                    mm(sums(0, 1), m[:, 192:320], moving(t, 3, 1), start=t == 0, stop=stop, skip_group_check=True)
                    mm(sums(1, 2), m[:, 64:192], moving(t, 0, 2), start=False, stop=stop, skip_group_check=True)
                    last = mm(sums(3, 2), m[:, 0:128], moving(t, 2, 2), start=False, stop=stop, skip_group_check=True)
                last.then_inc(s_agg[1], 1)

            def windows(l, s, j):
                count = pe.value_load(wtab[0:1, 1, bass.ds(s, 1)], min_val=1, max_val=WINDOWS)
                pair0 = pe.value_load(wtab[0:1, 2, bass.ds(s, 1)], min_val=PAIR0, max_val=PAIR0 + SUPS * WINDOWS)
                with pe.Fori(0, count) as k:
                    pair = pe.snap(pair0 + k)
                    pe.wait_ge(s_sel[l], pair)
                    (sum_pair0 if l == 0 else sum_pair1)(pair, j)

            def edge_layer(l):
                mm(bank(AGG)[:, 0:REG1 * WIN], ident[:], zeros[:], start=True, stop=True).then_inc(s_agg[l], 1)
                if l == 0:
                    radial0(0, 0, 0)
                else:
                    hidden1(0, 0, 0)
                    hidden1(1, 0, 1)
                    radial1(0, 0)

                def supertile(s, i, j, left=SUPS):
                    if l == 0:
                        if left > 1:
                            radial0(s + 1, i + (j + 1) // SLOTS, (j + 1) % SLOTS)
                    else:
                        if left > 2:
                            hidden1(s + 2, i + (j + 2) // SLOTS, (j + 2) % SLOTS)
                        if left > 1:
                            radial1(s + 1, (j + 1) % SLOTS)
                    windows(l, s, j)

                with pe.Fori(0, ROUNDS - 1) as i:
                    for j in range(SLOTS):
                        supertile(i * SLOTS + j, i, j)
                for j in range(SLOTS):
                    supertile((ROUNDS - 1) * SLOTS + j, ROUNDS - 1, j, SLOTS - j)

            edge_layer(0)

            def node_product0(g, first):
                if not first:
                    pe.wait_ge(s_ln[0], (g - 1) * LN_STEPS[0] + 2)
                for j in range(GROUP):
                    pe.wait_ge(s_stage[0], g * GROUP + j + 1)
                    mm(yps[:, j, 0:DIM], stage0[:, j, 0, :], la[:], start=True, stop=False)
                    mm(yps[:, j, 0:DIM], stage0[0:96, j, 1, :], lb[:], start=False, stop=True)
                    mm(yps[:, j, DIM:DIM + 1], stage0[0:1, j, 2, :], one[:], start=True, stop=True).then_inc(s_y[0], 1)

            def features(g, first):
                for j in range(GROUP):
                    n = g * GROUP + j
                    if j == 0:
                        pe.wait_ge(s_ln[0], (g + 1) * LN_STEPS[0])
                        if not first:
                            pe.wait_ge(s_fev, n)
                    else:
                        pe.wait_ge(s_tpe, n)
                    nc.tensor.transpose(tps_[j % 2][:, 0:P], og[:, j, 0:P], ident[:])
                    nc.tensor.transpose(tps_[j % 2][0:MV, P:2 * P], og[:, j, P:DIM], ident[:]).then_inc(s_tp, 1)
                    pe.wait_ge(s_tpe, n + 1)
                    if j >= 2:
                        pe.wait_ge(s_fev, n - 1)
                    x, f = xt1[:, j, :, :], fps[j % 2]

                    mm(f[:, 32:288], x[:, 0, :], wfa[:], start=True, stop=True)
                    mm(f[:, 0:32], x[0:32, 1, :], wfb[:, 0:32], start=True, stop=True)
                    mm(f[:, 288:320], x[0:32, 1, :], wfb[:, 32:64], start=True, stop=True).then_inc(s_f, 1)

            pe.wait_ge(s_done[0], 1)
            node_product0(0, True)
            node_product0(1, False)
            features(0, True)
            with pe.Fori(1, GROUPS - 1) as g:
                node_product0(g + 1, False)
                features(g, False)
            features(GROUPS - 1, False)

            pe.wait_ge(s_fev, GROUPS * GROUP)
            pe.wait_ge(s_ln[0], GROUPS * LN_STEPS[0])
            edge_layer(1)

            def node_product1(g, first):
                if not first:
                    pe.wait_ge(s_ln[1], (g - 1) * LN_STEPS[1] + 2)
                for j in range(GROUP):
                    pe.wait_ge(s_stage[1], g * GROUP + j + 1)
                    for r in range(REG1):
                        k = P if r < REG1 - 1 else MV
                        last = mm(yps[:, j, 0:DIM + 1], stage1[0:k, j, r, :], wout[0:k, r, :],
                                  start=r == 0, stop=r == REG1 - 1)
                    last.then_inc(s_y[1], 1)

            pe.wait_ge(s_done[1], 1)
            node_product1(0, True)
            with pe.Fori(1, GROUPS) as g:
                node_product1(g, False)


def kernel(x, src, dst, edge_attr_16, edge_attr_4, node_vec1, L0_gnn_W_ss, L0_gnn_W_sv, L0_gnn_W_vs, L0_gnn_W_vv,
           L0_gnn_W_rad, L0_gnn_b_rad, L0_gnn_L_s, L0_gnn_L_v, L1_gnn_Wfc1, L1_gnn_Wfc2, L1_gnn_Wsc0, L1_gnn_Wsc1,
           L1_gnn_Wl1_0, L1_gnn_Wl1_1, L1_gnn_Wl2_s, L1_gnn_Wl2_v, L1_gnn_Wa):
    import numpy as np
    import concourse.bacc as bacc
    from concourse.bass_utils import run_bass_kernel_spmd

    (x, src, dst, ea, sh, attr, wss, wsv, wvs, wvv, wr, br, ls, lv, fc1, fc2, sc0, sc1, l10, l11, l2s, l2v, wa) = (
        np.asarray(v) for v in (
            x, src, dst, edge_attr_16, edge_attr_4, node_vec1, L0_gnn_W_ss, L0_gnn_W_sv, L0_gnn_W_vs, L0_gnn_W_vv,
            L0_gnn_W_rad, L0_gnn_b_rad, L0_gnn_L_s, L0_gnn_L_v, L1_gnn_Wfc1, L1_gnn_Wfc2, L1_gnn_Wsc0, L1_gnn_Wsc1,
            L1_gnn_Wl1_0, L1_gnn_Wl1_1, L1_gnn_Wl2_s, L1_gnn_Wl2_v, L1_gnn_Wa))

    def placed(rows, cols, *blocks):
        out = np.zeros((rows, cols), blocks[0][2].dtype)
        for r, c, b in blocks:
            out[r:r + b.shape[0], c:c + b.shape[1]] = b
        return out

    s_of = np.arange(MS)
    v_of = [MS + 3 * np.arange(MV) + d for d in range(3)]
    by_component = np.concatenate([s_of, *v_of])
    by_row0 = np.concatenate([v_of[2], s_of, v_of[0], v_of[1]])
    xd = placed(NODES_PAD, DIM, (0, 0, x[:, by_component]))

    def by_supertile(v, fill):
        v = v.reshape(EDGES, -1)
        v = np.concatenate([v, np.full((EDGES_PAD - EDGES, v.shape[1]), fill, v.dtype)])
        return v.reshape(SUPS, TPS, P, -1).transpose(0, 2, 1, 3).reshape(SUPS, P, -1)

    dst_pad = by_supertile(dst, NODES_PAD - 1)
    sh_pad = by_supertile(sh[:, [1, 2, 3, 0]], 0)
    dsts = np.concatenate([dst, np.full(EDGES_PAD - EDGES, NODES_PAD - 1, dst.dtype)]).reshape(ROUNDS, SLOTS, SUP_EDGES)
    f2 = np.concatenate([fc2[:, 128:160], fc2[:, 160:192], fc2[:, 64:128], fc2[:, 0:64]], axis=1)
    n1 = (l2s[MS:], wa[MS:])
    V = [MS, MS + MV, MS + 2 * MV]
    wout = np.stack([
        placed(P, DIM + 1, (0, 0, l2s[:MS]), (0, DIM, wa[:MS]), (64, V[0], l2v[MS:]), (96, V[1], l2v[MS:])),
        placed(P, DIM + 1, (0, V[0], l2v[:MS]), (64, 0, n1[0]), (64, DIM, n1[1])),
        placed(P, DIM + 1, (0, V[1], l2v[:MS]), (96, 0, n1[0]), (96, DIM, n1[1])),
        placed(P, DIM + 1, (64, V[2], l2v[:MS]), (32, 0, n1[0]), (32, DIM, n1[1])),
        placed(P, DIM + 1, (0, V[2], l2v[MS:])),
    ], axis=1)
    ins = {
        "xT": xd.T, "xd": xd,
        "srcs": by_supertile(src, 0),
        "dst_sh": np.concatenate([dst_pad, sh_pad.view(np.int32)], axis=2),
        "dsts": dsts,
        "escal": placed(FIN, EDGES_PAD, (0, 0, ea.T)),
        "attr": placed(NODES_PAD, 1, (0, 0, attr)).reshape(NODE_TILES, P).T,
        "w0a": placed(P, 288, (0, 0, wss), (0, 64, wsv), (64, 96, wvv), (64, 160, wvs), (96, 192, wvv), (96, 256, wvs)),
        "w0b": placed(MV, 96, (0, 0, wvv), (0, 64, wvs)),
        "la": placed(P, DIM, (0, 0, ls), (64, V[0], lv), (96, V[1], lv)),
        "lb": placed(96, DIM, (0, 0, ls), (64, V[2], lv)),
        "wfa": placed(P, 256, (0, 0, l10), (64, 64, l11), (96, 96, l11), (0, 128, sc0), (64, 192, sc1), (96, 224, sc1)),
        "wfb": placed(MV, 2 * MV, (0, 0, l11), (0, 32, sc1)),
        "wrad": np.concatenate([wr.T[:, by_row0], br[None, by_row0]]),
        "fc1": fc1, "fc2": f2, "wout": wout,
    }
    nc = bacc.Bacc("TRN2", target_bir_lowering=False, num_devices=1)
    arrays, aps = {}, {}
    for name, v in ins.items():
        v = np.ascontiguousarray(v)
        arrays[f"in_{name}"] = v
        aps[name] = nc.dram_tensor(f"in_{name}", v.shape, mybir.dt.from_np(v.dtype), kind="ExternalInput").ap()
    aps["out"] = nc.dram_tensor("out_rows", (NODES_PAD, DIM), mybir.dt.float32, kind="ExternalOutput").ap()
    mk_gnn_resnorm_d2_gnn_r8_694f30_kernel(nc, aps)
    r = run_bass_kernel_spmd(nc, [arrays], core_ids=[0])
    return r.results[0]["out_rows"][:NODES]
```

```python
import concourse.bass as bass
from concourse import mybir
from contextlib import ExitStack

NODES, EDGES = 6250, 206250
MS, MV = 64, 32
DIM = MS + 3 * MV

P = 128
TPS = 4
SUP_EDGES = TPS * P
SLOTS = 4
SUPS = -(-EDGES // (SUP_EDGES * SLOTS)) * SLOTS
ROUNDS = SUPS // SLOTS
EDGES_PAD = SUPS * SUP_EDGES

GROUP = 7
NODE_TILES = -(-NODES // P)
GROUPS = NODE_TILES // GROUP
NODES_PAD = NODE_TILES * P
assert GROUPS * GROUP == NODE_TILES

FIN = 16
HID = 64
ROW0 = 448
ROW1 = 224
MSG0 = DIM + 1
MSG1 = 384
WEIGHTED = 544
EPS = 1e-5
BANK = 512


def mk_gnn_resnorm_d2_gnn_r8_694f30_kernel(nc, a):
    f32, i32, i16 = mybir.dt.float32, mybir.dt.int32, mybir.dt.int16
    ALU = mybir.AluOpType
    ACT = mybir.ActivationFunctionType
    AX = mybir.AxisListType
    ctx = ExitStack()
    with ctx:
        def sb(name, shape, dt=f32):
            return ctx.enter_context(nc.sbuf_tensor(name, shape, dt))

        def sem(name):
            return ctx.enter_context(nc.semaphore(name))

        arena = sb("arena", [P, NODE_TILES * MSG1])
        acc1 = arena[:, :].rearrange("p (w c) -> p w c", w=NODE_TILES)
        acc0 = sb("acc0", [P, NODE_TILES, MSG0])
        rows0 = arena[:, 0:SLOTS * TPS * ROW0].rearrange("p (s t c) -> p s t c", s=SLOTS, t=TPS)
        at = SLOTS * TPS * ROW0
        msg0 = arena[:, at:at + 2 * TPS * MSG0].rearrange("p (s t c) -> p s t c", s=2, t=TPS)
        work = sb("work", [P, TPS * (SLOTS * ROW1 + 2 * WEIGHTED + 2 * MSG1)])
        at1, at2 = SLOTS * TPS * ROW1, TPS * (SLOTS * ROW1 + 2 * WEIGHTED)
        rows1 = work[:, 0:at1].rearrange("p (s t c) -> p s t c", s=SLOTS, t=TPS)
        weighted = work[:, at1:at2].rearrange("p (s t c) -> p s t c", s=2, t=TPS)
        msg1 = work[:, at2:].rearrange("p (s t c) -> p s t c", s=2, t=TPS)

        def of_group(at, *shape):
            n = 1
            for d in shape:
                n *= d
            v = work[:, at:at + GROUP * n]
            return v.rearrange("p (g c) -> p g c", g=GROUP) if len(shape) == 1 else v.rearrange(
                "p (g h n) -> p g h n", g=GROUP, h=shape[0])

        xstage, trows = of_group(0, 2, P), of_group(GROUP * 2 * P, ROW0)
        stage0, ht, xt1, feat = (of_group(0, MSG0), of_group(1200, 2, P), of_group(3000, 2, P),
                                 of_group(4800, ROW1 + DIM))
        stage1, at3 = of_group(0, MSG1), of_group(GROUP * MSG1, MSG1)

        iota = sb("iota", [P, NODES_PAD], i16)
        srcs = sb("srcs", [P, SLOTS, TPS], i32)
        dst_sh = sb("dst_sh", [P, SLOTS, 5 * TPS], i32)
        escal = sb("escal", [FIN + 1, SLOTS, SUP_EDGES])
        hid = sb("hid", [2 * HID, 2, 2 * P])
        onehot = sb("onehot", [P, 3, TPS, P])
        half = sb("half", [P, TPS, 2, MS])
        total = sb("total", [P, 2, TPS, DIM])
        zeros = sb("zeros", [P, MSG1])
        ident = sb("ident", [P, P])
        attr = sb("attr", [P, NODE_TILES])
        gain = sb("gain", [P, NODE_TILES])
        after = [v[:, 0:4 * GROUP * DIM].rearrange("p (k g c) -> p k g c", k=4, g=GROUP)
                 for v in (arena[:, :], acc0[:, :, :].rearrange("p w c -> p (w c)"))]
        xg, tg, sq, og = ([v[:, k] for v in after] for k in range(4))
        stat = sb("stat", [P, 8, GROUP])
        wtab = sb("wtab", [1, 3, SUPS], i32)
        wtabf = arena[0:1, SLOTS * SUP_EDGES:SLOTS * SUP_EDGES + 4 * SUPS].rearrange("p (k s) -> p k s", k=4)
        wends = sb("wends", [ROUNDS, 2, SLOTS])
        dsts = arena[0:ROUNDS, 0:SLOTS * SUP_EDGES].bitcast(i32).rearrange("p (s e) -> p s e", s=SLOTS)
        w0a, w0b = sb("w0a", [P, ROW0]), sb("w0b", [MV, 96])
        la, lb = sb("la", [P, DIM]), sb("lb", [MV, DIM])
        wfa, wfb = sb("wfa", [P, ROW1 + DIM]), sb("wfb", [MV, 2 * MV])
        wrad = sb("wrad", [FIN + 1, DIM])
        fc1, fc2 = sb("fc1", [FIN, HID]), sb("fc2", [2 * HID, 192])
        wout = sb("wout", [P, 3, DIM + 1])

        ps = ctx.enter_context(nc.psum_tensor("ps", [P, 8 * BANK], f32))

        def bank(b, n=1):
            return ps[:, b * BANK:(b + n) * BANK]

        def two_to_a_bank(b, n):
            return bank(b, 2).rearrange("p (t c) -> p t c", t=TPS)[:, :, 0:n]

        rad = [two_to_a_bank(2 * b, DIM) for b in range(2)]
        wps = [two_to_a_bank(2 * b, 192) for b in range(2)]
        FIRST, MORE = 4, 6
        hps = bank(7)
        yps = bank(0, 4).rearrange("p (g c) -> p g c", c=BANK // 2)
        tps_, fps = [bank(4), bank(5)], [bank(6), bank(7)]

        def dram(name, shape):
            return nc.dram_tensor(name, shape, f32, kind="Internal").ap()

        table0, table1 = dram("table0", [NODES_PAD, ROW0]), dram("table1", [NODES_PAD, ROW1])
        base_d, wends_d = dram("base_d", [NODES_PAD, DIM]), dram("wends_d", [2, SUPS])

        def node_rows(t, g):
            return t[bass.ds(g * (GROUP * P), GROUP * P), :].rearrange("(g p) c -> p g c", p=P)

        s_weights, s_wscaled = sem("weights_loaded"), sem("weights_scaled")
        s_const = sem("constants_made")
        s_dsts, s_ends, s_endsout, s_endsin = sem("dsts_loaded"), sem("ends_found"), sem("ends_stored"), sem("ends_loaded")
        s_wstep, s_wtab = sem("window_step"), sem("window_table_made")
        s_zero0, s_zero1, s_acc0x = sem("sums0_zeroed"), sem("sums1_zeroed"), sem("sums0_have_x")
        s_xst = [sem(f"x_tile_loaded{j}") for j in range(GROUP)]
        s_tmm, s_tev, s_tst = sem("table0_product"), [sem("table0_by_act"), sem("table0_by_dve")], [sem(f"table0_stored{j}") for j in range(GROUP)]
        s_src = [[sem(f"srcs_loaded{l}_{j}") for j in range(SLOTS)] for l in range(2)]
        s_dsh = [[sem(f"dst_sh_loaded{l}_{j}") for j in range(SLOTS)] for l in range(2)]
        s_esc = [[sem(f"edge_scalars_loaded{l}_{j}") for j in range(SLOTS)] for l in range(2)]
        s_rows = [[sem(f"rows_gathered{l}_{j}") for j in range(SLOTS)] for l in range(2)]
        s_pool = sem("pool_went_on")
        s_lin, s_act = [sem(f"radial_product{l}") for l in range(2)], [sem(f"radial_activated{l}") for l in range(2)]
        s_w2 = sem("radial_weights")
        s_msg = [sem(f"messages_made{l}") for l in range(2)]
        s_wtd = [sem(f"rows_weighted{l}") for l in range(2)]
        s_ev2 = [sem(f"rows_weighted_by_ev2_{l}") for l in range(2)]
        s_part = [sem(f"message_part{l}") for l in range(2)]
        s_oh, s_ohx = [sem(f"first_onehot{l}") for l in range(2)], [sem(f"more_onehot{l}") for l in range(2)]
        s_agg, s_aggx = [sem(f"first_summed{l}") for l in range(2)], [sem(f"more_summed{l}") for l in range(2)]
        s_add, s_addx = [sem(f"first_added{l}") for l in range(2)], [sem(f"more_added{l}") for l in range(2)]
        s_done = [sem(f"sums_complete{l}") for l in range(2)]
        s_xin, s_xin1 = sem("x_rows_loaded"), sem("base_rows_loaded")
        s_stage, s_y = [sem(f"sums_staged{l}") for l in range(2)], [sem(f"node_product{l}") for l in range(2)]
        s_ln, s_lnact = [sem(f"norm_step{l}") for l in range(2)], [sem(f"norm_act{l}") for l in range(2)]
        s_ht, s_hte = [sem(f"sums_transposed{l}") for l in range(2)], [sem(f"sums_t_copied{l}") for l in range(2)]
        s_tp, s_tpe, s_f, s_fev = sem("x1_transposed"), sem("x1t_copied"), sem("features"), sem("features_copied")
        s_base, s_fst, s_out = sem("base_ready"), sem("table1_stored"), sem("out_stored")

        WEIGHTS = [(w0a, "w0a"), (w0b, "w0b"), (la, "la"), (lb, "lb"), (wfa, "wfa"), (wfb, "wfb"),
                   (wrad, "wrad"), (fc1, "fc1"), (fc2, "fc2"), (wout, "wout"), (attr, "attr")]
        ISQ3, ISQ2 = 3.0 ** -0.5, 2.0 ** -0.5
        I8, I32, I96 = MS ** -0.5, MV ** -0.5, (MS + MV) ** -0.5
        SCALED = [(w0a[0:64, 0:64], I8 * ISQ2), (w0a[0:64, 160:448], I8 * ISQ3 * ISQ2),
                  (w0a[64:128, :], I32 * ISQ3 * ISQ2), (w0b[:], I32 * ISQ3 * ISQ2),
                  (la[0:64, :], I8), (la[64:128, :], I32), (lb[:], I32),
                  (wfa[0:64, :], I8), (wfa[64:128, :], I32), (wfb[:], I32),
                  (fc1[:], FIN ** -0.5), (fc2[:], HID ** -0.5),
                  (wout[:, 0:2, :], I96), (wout[0:96, 2, :], I96), (wout[96:128, 2, :], I96 * ISQ3)]
        ARENA_HALF = NODE_TILES * MSG1 // 2
        LN_STEPS = [12, 11]
        block = ctx.enter_context(nc.Block())

        @block.sync
        def _(sp):
            sp.dma_start(dsts, a["dsts"]).then_inc(s_dsts, 16)
            for t, name in WEIGHTS:
                sp.dma_start(t[:], a[name]).then_inc(s_weights, 16)

            def load_x(g, j):
                at = g * (GROUP * P) + j * P
                sp.dma_start(xstage[:, j, 0, :], a["xT"][0:P, bass.ds(at, P)]).then_inc(s_xst[j], 16)
                sp.dma_start(xstage[0:MV, j, 1, :], a["xT"][P:DIM, bass.ds(at, P)]).then_inc(s_xst[j], 16)

            for j in range(GROUP):
                load_x(0, j)
            sp.dma_start(acc0[:, :, 0:DIM], a["xd"].rearrange("(w p) c -> p w c", p=P)).then_inc(s_acc0x, 16)
            sp.wait_ge(s_ends, 2)
            for e in range(2):
                sp.dma_start(wends_d[e:e + 1, :].rearrange("o (p s) -> (o p) s", s=SLOTS),
                             wends[:, e, :]).then_inc(s_endsout, 16)
            sp.wait_ge(s_endsout, 32)
            sp.dma_start(wtabf[:, 0:2, :], wends_d.rearrange("(o e) s -> o e s", o=1)).then_inc(s_endsin, 16)

            def store_row(g, j):
                by, of = j % 2, (GROUP + 1 - j % 2) // 2
                sp.wait_ge(s_tev[by], g * of + j // 2 + 1)
                at = g * (GROUP * P) + j * P
                sp.dma_start(table0[bass.ds(at, P), :], trows[:, j, :]).then_inc(s_tst[j], 16)

            with sp.Fori(0, GROUPS - 1) as g:
                for j in range(GROUP):
                    store_row(g, j)
                    load_x(g + 1, j)
            for j in range(GROUP):
                store_row(GROUPS - 1, j)

            def load_src(l, s, j):
                sp.dma_start(srcs[:, j, :], a["srcs"][bass.ds(s, 1), :, :].rearrange("o p c -> (o p) c")).then_inc(s_src[l][j], 16)

            def load_dst_sh(l, s, j):
                sp.dma_start(dst_sh[:, j, :], a["dst_sh"][bass.ds(s, 1), :, :].rearrange("o p c -> (o p) c")).then_inc(s_dsh[l][j], 16)

            def load_escal(l, s, j):
                sp.dma_start(escal[0:FIN, j, :], a["escal"][:, bass.ds(s * SUP_EDGES, SUP_EDGES)]).then_inc(s_esc[l][j], 16)

            for l in range(2):
                if l == 0:
                    sp.wait_ge(s_const, 4)
                else:
                    sp.wait_ge(s_done[0], 1)
                for j in range(SLOTS):
                    load_src(l, j, j)
                    load_escal(l, j, j)
                    load_dst_sh(l, j, j)
                with sp.Fori(0, ROUNDS - 1) as i:
                    for j in range(SLOTS):
                        s = i * SLOTS + j
                        sp.wait_ge(s_rows[l][j], (i + 1) * 16 * TPS)
                        load_src(l, s + SLOTS, j)
                        sp.wait_ge(s_lin[l], s + 1)
                        load_escal(l, s + SLOTS, j)
                        sp.wait_ge(s_msg[l], s + 2)
                        load_dst_sh(l, s + SLOTS, j)
                if l == 0:
                    sp.dma_start(xg[0], node_rows(a["xd"], 0)).then_inc(s_xin, 16)
                    def store_features(g):
                        sp.wait_ge(s_base, g + 1)
                        sp.dma_start(node_rows(table1, g), feat[:, :, 0:ROW1]).then_inc(s_fst, 16)
                        sp.dma_start(node_rows(base_d, g), feat[:, :, ROW1:]).then_inc(s_fst, 16)

                    with sp.Fori(0, GROUPS - 1) as g:
                        sp.wait_ge(s_ln[0], g * LN_STEPS[0] + 1)
                        sp.dma_start(xg[0], node_rows(a["xd"], g + 1)).then_inc(s_xin, 16)
                        store_features(g)
                    store_features(GROUPS - 1)

            sp.wait_ge(s_fst, 32 * GROUPS)
            sp.wait_ge(s_ln[0], GROUPS * LN_STEPS[0])
            sp.dma_start(xg[1], node_rows(base_d, 0)).then_inc(s_xin1, 16)

            def store_out(g):
                sp.wait_ge(s_ln[1], (g + 1) * LN_STEPS[1])
                sp.dma_start(node_rows(a["out"], g), og[1]).then_inc(s_out, 16)

            with sp.Fori(0, GROUPS - 1) as g:
                sp.wait_ge(s_ln[1], g * LN_STEPS[1] + 3)
                sp.dma_start(xg[1], node_rows(base_d, g + 1)).then_inc(s_xin1, 16)
                store_out(g)
            store_out(GROUPS - 1)
            sp.wait_ge(s_out, 16 * GROUPS)

        @block.gpsimd
        def _(pool):
            nc.gpsimd.memset(zeros[:], 0.0).then_inc(s_const, 1)
            nc.gpsimd.memset(ident[:], 0.0).then_inc(s_const, 1)
            nc.gpsimd.memset(escal[:], 1.0).then_inc(s_const, 1)
            pool.wait_ge(s_const, 2)
            nc.gpsimd.affine_select(out=ident[:], in_=ident[:], compare_op=ALU.not_equal, fill=1.0, base=0,
                                    pattern=[[-1, P]], channel_multiplier=1).then_inc(s_const, 1)
            nc.gpsimd.iota(iota[:], pattern=[[1, NODES_PAD]], base=0, channel_multiplier=0).then_inc(s_const, 1)
            nc.gpsimd.memset(msg0[:, :, :, DIM:MSG0], 1.0).then_inc(s_zero0, 1)
            nc.gpsimd.memset(acc0[:, :, DIM:MSG0], 0.0).then_inc(s_zero0, 1)

            def gather(l, j):
                rows, table = (rows0, table0) if l == 0 else (rows1, table1)
                for t in range(TPS):
                    pool.indirect_dma_start(
                        out=rows[:, j, t, :], out_offset=None, in_=table,
                        in_offset=bass.IndirectOffsetOnAxis(ap=srcs[:, j, t:t + 1], axis=0)).then_inc(s_rows[l][j], 16)

            def gathers(l):
                for j in range(SLOTS):
                    pool.wait_ge(s_src[l][j], 16)
                    gather(l, j)
                if l == 1:
                    nc.gpsimd.memset(arena[:, ARENA_HALF:], 0.0).then_inc(s_zero1, 1)
                with pool.Fori(0, ROUNDS - 1) as i:
                    for j in range(SLOTS):
                        s = i * SLOTS + j
                        pool.wait_ge(s_wtd[l], s + 1)
                        pool.sem_inc(s_pool, 1)
                        pool.wait_ge(s_ev2[l], s + 1)
                        pool.sem_inc(s_pool, 1)
                        pool.wait_ge(s_src[l][j], (i + 2) * 16)
                        pool.sem_inc(s_pool, 1)
                        gather(l, j)

            def stage(l, g, j, first):
                if not first:
                    pool.wait_ge(s_ht[l], (g - 1) * GROUP + j + 1)
                    if l == 0 and j == 0:
                        pool.wait_ge(s_ln[0], (g - 1) * LN_STEPS[0] + 2)
                acc, to = (acc0, stage0) if l == 0 else (acc1, stage1)
                nc.gpsimd.tensor_copy(to[:, j, :], acc[:, bass.ds(g * GROUP + j, 1), :].rearrange("p o c -> p (o c)")).then_inc(s_stage[l], 1)

            for j in range(GROUP):
                pool.wait_ge(s_tst[j], 16 * GROUPS)
            gathers(0)

            pool.wait_ge(s_done[0], 1)
            for j in range(GROUP):
                stage(0, 0, j, True)

            def base(g):
                pool.wait_ge(s_fev, (g + 1) * GROUP)
                pool.wait_ge(s_ln[0], (g + 1) * LN_STEPS[0])
                nc.gpsimd.tensor_tensor(feat[:, :, ROW1:], feat[:, :, ROW1:], og[0], ALU.add).then_inc(s_base, 1)

            with pool.Fori(0, GROUPS - 1) as g:
                for j in range(GROUP):
                    stage(0, g + 1, j, False)
                base(g)
            base(GROUPS - 1)

            pool.wait_ge(s_fst, 32 * GROUPS)
            gathers(1)
            pool.wait_ge(s_done[1], 1)
            for j in range(GROUP):
                stage(1, 0, j, True)
            with pool.Fori(1, GROUPS) as g:
                for j in range(GROUP):
                    stage(1, g, j, False)

        @block.scalar
        def _(act):
            def table_row(g, j, first):
                act.wait_ge(s_tmm, g * GROUP + j + 1)
                if not first:
                    act.wait_ge(s_tst[j], g * 16)
                nc.scalar.activation(trows[:, j, :], bank(j)[:, 0:ROW0], ACT.Copy).then_inc(s_tev[0], 1)

            for j in range(0, GROUP, 2):
                table_row(0, j, True)
            with act.Fori(1, GROUPS) as g:
                for j in range(0, GROUP, 2):
                    table_row(g, j, False)

            def weight_rows(l, s, i, j, first):
                if not first or j >= 2:
                    act.wait_ge(s_msg[l], s - 1)
                act.wait_ge(s_rows[l][j], (i + 1) * 16 * TPS)
                act.wait_ge(s_dsh[l][j], (i + 1) * 16)
                r, u = (rows0, rows1)[l][:, j, :, :], weighted[:, j % 2, :, :]
                parts = ([(0, 160, 256, 160), (1, 256, 352, 256), (3, 0, 160, 0)],
                         [(0, 0, 96, 224), (1, 32, 128, 352), (3, 0, 224, 0)])[l]
                for t in range(TPS):
                    for k, c0, c1, to in parts:
                        at = TPS + 4 * t + k
                        last = nc.scalar.activation(u[:, t, to:to + c1 - c0], r[:, t, c0:c1], ACT.Copy,
                                                    scale=dst_sh[:, j, at:at + 1].bitcast(f32))
                last.then_inc(s_wtd[l], 1)

            def supertile0(s, i, j, first):
                weight_rows(0, s, i, j, first)
                act.wait_ge(s_lin[0], s + 1)
                nc.scalar.activation(rad[j % 2], rad[j % 2], ACT.Sigmoid).then_inc(s_act[0], 1)

            for j in range(SLOTS):
                supertile0(j, 0, j, True)
            with act.Fori(1, ROUNDS) as i:
                for j in range(SLOTS):
                    supertile0(i * SLOTS + j, i, j, False)

            def transposed(l, g):
                for j in range(GROUP):
                    act.wait_ge(s_ht[l], g * GROUP + j + 1)
                    if l == 0:
                        nc.scalar.activation(ht[:, j, 0, :], tps_[j % 2][:, 0:P], ACT.Copy)
                        nc.scalar.activation(ht[0:MV, j, 1, :], tps_[j % 2][0:MV, P:2 * P], ACT.Copy).then_inc(s_hte[0], 1)
                    else:
                        nc.scalar.activation(at3[:, j, :], tps_[j % 2][:, 0:MSG1], ACT.Copy).then_inc(s_hte[1], 1)

            def norm_act(l, g, square_at, sqrt_at):
                act.wait_ge(s_ln[l], g * LN_STEPS[l] + square_at)
                nc.scalar.activation(sq[l], tg[l], ACT.Square).then_inc(s_lnact[l], 1)
                act.wait_ge(s_ln[l], g * LN_STEPS[l] + sqrt_at)
                nc.scalar.activation(stat[:, 6, :], stat[:, 5, :], ACT.Sqrt).then_inc(s_lnact[l], 1)

            def features(g, first):
                if not first:
                    act.wait_ge(s_fst, g * 32)
                for j in range(GROUP):
                    n = g * GROUP + j
                    act.wait_ge(s_tp, n + 1)
                    nc.scalar.activation(xt1[:, j, 0, :], tps_[j % 2][:, 0:P], ACT.Copy)
                    nc.scalar.activation(xt1[0:MV, j, 1, :], tps_[j % 2][0:MV, P:2 * P], ACT.Copy).then_inc(s_tpe, 1)
                    act.wait_ge(s_f, n + 1)
                    nc.scalar.activation(feat[:, j, :], fps[j % 2][:, 0:ROW1 + DIM], ACT.Copy,
                                         scale=attr[:, bass.ds(n, 1)]).then_inc(s_fev, 1)

            transposed(0, 0)
            transposed(0, 1)
            norm_act(0, 0, 8, 10)
            features(0, True)
            with act.Fori(1, GROUPS - 1) as g:
                transposed(0, g + 1)
                norm_act(0, g, 8, 10)
                features(g, False)
            norm_act(0, GROUPS - 1, 8, 10)
            features(GROUPS - 1, False)

            def silu(s, j):
                act.wait_ge(s_lin[1], s + 1)
                nc.scalar.activation(hid[:, j % 2, :], hps[:, 0:2 * P], ACT.Silu).then_inc(s_act[1], 1)

            def supertile1(s, i, j, first=False, left=SUPS):
                weight_rows(1, s, i, j, first)
                if left > 1:
                    silu(s + 1, j + 1)

            silu(0, 0)
            for j in range(SLOTS):
                supertile1(j, 0, j, first=True)
            with act.Fori(1, ROUNDS - 1) as i:
                for j in range(SLOTS):
                    supertile1(i * SLOTS + j, i, j)
            for j in range(SLOTS):
                supertile1((ROUNDS - 1) * SLOTS + j, ROUNDS - 1, j, left=SLOTS - j)

            transposed(1, 0)
            with act.Fori(0, GROUPS - 1) as g:
                transposed(1, g + 1)
                norm_act(1, g, 6, 8)
            norm_act(1, GROUPS - 1, 6, 8)

        @block.vector
        def _(dve):
            dve.wait_ge(s_dsts, 16)
            nc.vector.tensor_reduce(wends[:, 0, :], dsts, AX.X, ALU.min).then_inc(s_ends, 1)
            nc.vector.tensor_reduce(wends[:, 1, :], dsts, AX.X, ALU.max).then_inc(s_ends, 1)
            dve.wait_ge(s_weights, 16 * len(WEIGHTS))
            for w, c in SCALED:
                nc.vector.tensor_scalar(w, w, c, None, ALU.mult).then_inc(s_wscaled, 1)
            dve.wait_ge(s_endsin, 16)
            nc.vector.tensor_copy(wtab[:, 0:2, :], wtabf[:, 0:2, :]).then_inc(s_wstep, 1)
            dve.wait_ge(s_wstep, 1)
            nc.vector.tensor_scalar(wtab[:, 0:2, :], wtab[:, 0:2, :], P.bit_length() - 1, None,
                                    ALU.arith_shift_right).then_inc(s_wstep, 1)
            dve.wait_ge(s_wstep, 2)
            nc.vector.tensor_copy(wtabf[:, 0:2, :], wtab[:, 0:2, :]).then_inc(s_wstep, 1)
            dve.wait_ge(s_wstep, 3)
            nc.vector.tensor_tensor(wtabf[:, 1, :], wtabf[:, 1, :], wtabf[:, 0, :], ALU.subtract).then_inc(s_wstep, 1)
            dve.wait_ge(s_wstep, 4)
            nc.vector.tensor_tensor_scan(wtabf[:, 2, :], wtabf[:, 1, :], wtabf[:, 1, :], 1.0,
                                         ALU.add, ALU.bypass).then_inc(s_wstep, 1)
            dve.wait_ge(s_wstep, 5)
            nc.vector.tensor_tensor(wtabf[:, 3, :], wtabf[:, 2, :], wtabf[:, 1, :], ALU.subtract).then_inc(s_wstep, 1)
            dve.wait_ge(s_wstep, 6)
            nc.vector.tensor_copy(wtab[:, 1, :], wtabf[:, 1, :]).then_inc(s_wtab, 1)
            nc.vector.tensor_copy(wtab[:, 2, :], wtabf[:, 3, :]).then_inc(s_wtab, 1)

            def table_row(g, j, first):
                dve.wait_ge(s_tmm, g * GROUP + j + 1)
                if not first:
                    dve.wait_ge(s_tst[j], g * 16)
                nc.vector.tensor_copy(trows[:, j, :], bank(j)[:, 0:ROW0]).then_inc(s_tev[1], 1)

            for j in range(1, GROUP, 2):
                table_row(0, j, True)
            with dve.Fori(1, GROUPS) as g:
                for j in range(1, GROUP, 2):
                    table_row(g, j, False)

            def bc(x, axis, shape):
                return x.unsqueeze(axis).to_broadcast(shape)

            def weight_by_ev2(l, s, i, j):
                dve.wait_ge(s_rows[l][j], (i + 1) * 16 * TPS)
                dve.wait_ge(s_dsh[l][j], (i + 1) * 16)
                r, (c0, to) = (rows0, rows1)[l], ((352, 352), (128, 448))[l]
                ev2 = dst_sh[:, j, TPS:].bitcast(f32).rearrange("p (t k) -> p t k", k=4)[:, :, 2]
                nc.vector.tensor_tensor(weighted[:, j % 2, :, to:to + 96], r[:, j, :, c0:c0 + 96],
                                        bc(ev2, 2, [P, TPS, 96]), ALU.mult).then_inc(s_ev2[l], 1)

            def messages0(s, j):
                u, m, c, h, a = weighted[:, j % 2, :, :], msg0[:, j % 2, :, :], rad[j % 2], half, total[:, j % 2, :, :]

                def blocks(x, n):
                    return x.rearrange("p t (k c) -> p t k c", k=n)

                dve.wait_ge(s_ev2[0], s + 1)
                dve.wait_ge(s_wtd[0], s + 1)
                nc.vector.tensor_tensor(h[:], blocks(u[:, :, 0:512], 2)[:, :, :, 0:MS],
                                        blocks(u[:, :, 160:544], 2)[:, :, :, 0:MS], ALU.add).then_inc(s_part[0], 1)
                nc.vector.tensor_tensor(blocks(a[:, :, MS:DIM], 3), blocks(u[:, :, MS:DIM], 3),
                                        blocks(u[:, :, 160:448], 3)[:, :, :, MS:96], ALU.add).then_inc(s_part[0], 1)
                dve.wait_ge(s_part[0], s * 3 + 1)
                nc.vector.tensor_tensor(a[:, :, 0:MS], h[:, :, 0, :], h[:, :, 1, :], ALU.add).then_inc(s_part[0], 1)
                dve.wait_ge(s_part[0], s * 3 + 3)
                dve.wait_ge(s_act[0], s + 1)
                nc.vector.tensor_tensor(m[:, :, 0:DIM], a, c, ALU.mult).then_inc(s_msg[0], 1)

            def messages1(s, j):
                u, m, w, h = weighted[:, j % 2, :, :], msg1[:, j % 2, :, :], wps[j % 2], half

                def blocks(x, n):
                    return x.rearrange("p t (k c) -> p t k c", k=n)

                dve.wait_ge(s_ev2[1], s + 1)
                dve.wait_ge(s_wtd[1], s + 1)
                nc.vector.tensor_tensor(h[:, :, 0, 0:MV], u[:, :, 224:256], u[:, :, 416:448], ALU.add).then_inc(s_part[1], 1)
                dve.wait_ge(s_w2, s + 1)
                nc.vector.tensor_tensor(m[:, :, 0:MS], u[:, :, 32:96], w[:, :, 0:64], ALU.mult)
                nc.vector.tensor_tensor(blocks(m[:, :, 64:160], 3), blocks(u[:, :, 0:288], 3)[:, :, :, 0:MV],
                                        bc(w[:, :, 128:160], 2, [P, TPS, 3, MV]), ALU.mult)
                dve.wait_ge(s_part[1], s * 2 + 1)
                nc.vector.tensor_tensor(h[:, :, 1, 0:MV], h[:, :, 0, 0:MV], u[:, :, 512:544], ALU.add).then_inc(s_part[1], 1)
                nc.vector.tensor_tensor(blocks(m[:, :, 160:352], 3), blocks(u[:, :, 256:544], 3)[:, :, :, 0:MS],
                                        bc(w[:, :, 64:128], 2, [P, TPS, 3, MS]), ALU.mult)
                dve.wait_ge(s_part[1], s * 2 + 2)
                nc.vector.tensor_tensor(m[:, :, 352:384], h[:, :, 1, 0:MV], w[:, :, 160:192], ALU.mult).then_inc(s_msg[1], 1)

            def select(j, b, window):
                return nc.vector.tensor_tensor(onehot[:, b, :, :], bc(iota[:, bass.ds(window * P, P)], 1, [P, TPS, P]),
                                               bc(dst_sh[:, j, 0:TPS], 2, [P, TPS, P]), ALU.is_equal)

            def add_sums(l, b, window):
                acc, n = (acc0, MSG0) if l == 0 else (acc1, MSG1)
                to = acc[:, bass.ds(window, 1), :].rearrange("p o c -> p (o c)")
                return nc.vector.tensor_tensor(to, to, bank(b)[:, 0:n], ALU.add)

            def edge_layer(l):
                LAST = NODE_TILES - 1
                waiting, newer = dve.alloc_register(f"window_to_add{l}"), dve.alloc_register(f"window_after{l}")
                waiting_more = dve.alloc_register(f"more_to_add{l}")

                def held(register):
                    return dve.snap(register, min_val=0, max_val=LAST)

                dve.reg_mov(waiting, 0)
                dve.reg_mov(newer, 0)
                dve.reg_mov(waiting_more, 0)
                dve.sem_inc(s_add[l], 1)
                dve.sem_inc(s_addx[l], 1)

                def supertile(s, i, j):
                    window = dve.value_load(wtab[0:1, 0, bass.ds(s, 1)], min_val=0, max_val=LAST)
                    more = dve.value_load(wtab[0:1, 1, bass.ds(s, 1)], min_val=0, max_val=LAST)
                    dve.wait_ge(s_agg[l], s + 1)
                    dve.wait_ge(s_add[l], s + 1)
                    add_sums(l, FIRST + j % 2, held(waiting)).then_inc(s_add[l], 1)
                    weight_by_ev2(l, s, i, j)
                    select(j, j % 2, window).then_inc(s_oh[l], 1)
                    (messages0, messages1)[l](s, j)
                    with dve.If(more > 0):
                        first = dve.value_load(wtab[0:1, 2, bass.ds(s, 1)], min_val=1, max_val=SUPS * NODE_TILES)
                        with dve.Fori(0, more) as k:
                            e = dve.snap(first + k)
                            dve.wait_ge(s_aggx[l], e)
                            dve.wait_ge(s_addx[l], e)
                            dve.wait_ge(s_add[l], s + 2)
                            add_sums(l, MORE, held(waiting_more)).then_inc(s_addx[l], 1)
                            at = dve.snap(window + k + 1).with_bounds(min_val=1, max_val=LAST)
                            dve.wait_ge(s_addx[l], e + 1)
                            select(j, 2, at).then_inc(s_ohx[l], 1)
                            dve.reg_mov(waiting_more, at)
                    dve.reg_mov(waiting, held(newer))
                    dve.reg_mov(newer, window)

                with dve.Fori(0, ROUNDS) as i:
                    for j in range(SLOTS):
                        supertile(i * SLOTS + j, i, j)
                for k, window in enumerate((waiting, newer)):
                    dve.wait_ge(s_agg[l], SUPS + k + 1)
                    dve.wait_ge(s_add[l], SUPS + k + 1)
                    add_sums(l, FIRST + k, held(window)).then_inc(s_add[l], 1)
                first = dve.value_load(wtab[0:1, 2, SUPS - 1:SUPS], min_val=1, max_val=SUPS * NODE_TILES)
                more = dve.value_load(wtab[0:1, 1, SUPS - 1:SUPS], min_val=0, max_val=LAST)
                e = dve.snap(first + more)
                dve.wait_ge(s_aggx[l], e)
                dve.wait_ge(s_addx[l], e)
                dve.wait_ge(s_add[l], SUPS + 3)
                add_sums(l, MORE, held(waiting_more)).then_inc(s_addx[l], 1)
                dve.wait_ge(s_addx[l], e + 1)
                dve.sem_inc(s_done[l], 1)

            dve.wait_ge(s_const, 5)
            dve.wait_ge(s_zero0, 2)
            dve.wait_ge(s_acc0x, 16)
            dve.wait_ge(s_wtab, 2)
            edge_layer(0)

            def norm(l, g, n):
                base = g * LN_STEPS[l] + n
                dve.wait_ge(s_ln[l], base)
                nc.vector.tensor_reduce(stat[:, 3, :], tg[l], AX.X, ALU.add, negate=True).then_inc(s_ln[l], 1)
                dve.wait_ge(s_ln[l], base + 1)
                nc.vector.tensor_scalar(stat[:, 4, :], stat[:, 3, :], 1.0 / DIM, None, ALU.mult).then_inc(s_ln[l], 1)
                dve.wait_ge(s_ln[l], base + 2)
                nc.vector.tensor_tensor(tg[l], tg[l], bc(stat[:, 4, :], 2, [P, GROUP, DIM]), ALU.add).then_inc(s_ln[l], 1)
                dve.wait_ge(s_lnact[l], g * 2 + 1)
                nc.vector.tensor_reduce(stat[:, 0, :], sq[l], AX.X, ALU.add).then_inc(s_ln[l], 1)
                dve.wait_ge(s_ln[l], base + 4)
                nc.vector.tensor_scalar(stat[:, 5, :], stat[:, 0, :], 1.0 / DIM, EPS, ALU.mult, ALU.add).then_inc(s_ln[l], 1)
                dve.wait_ge(s_lnact[l], g * 2 + 2)
                nc.vector.reciprocal(stat[:, 7, :], stat[:, 6, :]).then_inc(s_ln[l], 1)
                dve.wait_ge(s_ln[l], base + 6)

            def nodes0(g, first):
                base = g * LN_STEPS[0]
                dve.wait_ge(s_y[0], (g + 1) * GROUP)
                dve.wait_ge(s_xin, (g + 1) * 16)
                if not first:
                    dve.wait_ge(s_ln[0], base)
                nc.vector.tensor_tensor(tg[0], yps[:, 0:GROUP, 0:DIM], xg[0], ALU.add).then_inc(s_ln[0], 1)
                dve.wait_ge(s_stage[0], (g + 1) * GROUP)
                nc.vector.tensor_scalar(stat[:, 0, :], stage0[:, :, DIM], 1.0, None, ALU.max).then_inc(s_ln[0], 1)
                dve.wait_ge(s_ln[0], base + 2)
                nc.vector.reciprocal(stat[:, 1, :], stat[:, 0, :]).then_inc(s_ln[0], 1)
                dve.wait_ge(s_ln[0], base + 3)
                nc.vector.tensor_tensor(stat[:, 2, :], stat[:, 1, :], attr[:, bass.ds(g * GROUP, GROUP)], ALU.mult).then_inc(s_ln[0], 1)
                dve.wait_ge(s_ln[0], base + 4)
                nc.vector.tensor_tensor(gain[:, bass.ds(g * GROUP, GROUP)], stat[:, 2, :], stat[:, 2, :], ALU.mult).then_inc(s_ln[0], 1)
                norm(0, g, 5)
                if not first:
                    dve.wait_ge(s_base, g)
                nc.vector.tensor_tensor(og[0], tg[0], bc(stat[:, 7, :], 2, [P, GROUP, DIM]), ALU.mult).then_inc(s_ln[0], 1)

            nodes0(0, True)
            with dve.Fori(1, GROUPS) as g:
                nodes0(g, False)

            dve.wait_ge(s_stage[0], GROUPS * GROUP)
            dve.wait_ge(s_fst, 32 * GROUPS)
            nc.vector.memset(arena[:, 0:ARENA_HALF], 0.0).then_inc(s_zero1, 1)
            dve.wait_ge(s_zero1, 2)
            edge_layer(1)

            def nodes1(g, first):
                base = g * LN_STEPS[1]
                dve.wait_ge(s_y[1], (g + 1) * GROUP)
                if not first:
                    dve.wait_ge(s_ln[1], base)
                nc.vector.tensor_tensor(stat[:, 0, :], yps[:, 0:GROUP, DIM], gain[:, bass.ds(g * GROUP, GROUP)], ALU.mult).then_inc(s_ln[1], 1)
                dve.wait_ge(s_ln[1], base + 1)
                nc.vector.tensor_tensor(tg[1], yps[:, 0:GROUP, 0:DIM], bc(stat[:, 0, :], 2, [P, GROUP, DIM]), ALU.mult).then_inc(s_ln[1], 1)
                dve.wait_ge(s_xin1, (g + 1) * 16)
                dve.wait_ge(s_ln[1], base + 2)
                nc.vector.tensor_tensor(tg[1], tg[1], xg[1], ALU.add).then_inc(s_ln[1], 1)
                norm(1, g, 3)
                if not first:
                    dve.wait_ge(s_out, g * 16)
                nc.vector.tensor_tensor(og[1][:, :, 0:MS], tg[1][:, :, 0:MS], bc(stat[:, 7, :], 2, [P, GROUP, MS]), ALU.mult).then_inc(s_ln[1], 1)
                nc.vector.tensor_tensor(og[1][:, :, MS:DIM].rearrange("p g (v d) -> p g d v", d=3),
                                        tg[1][:, :, MS:DIM].rearrange("p g (d v) -> p g d v", d=3),
                                        bc(stat[:, 7, :].unsqueeze(2), 3, [P, GROUP, 3, MV]), ALU.mult).then_inc(s_ln[1], 1)

            nodes1(0, True)
            with dve.Fori(1, GROUPS) as g:
                nodes1(g, False)

        @block.tensor
        def _(pe):
            mm = nc.tensor.matmul
            pe.wait_ge(s_wscaled, len(SCALED))
            pe.wait_ge(s_const, 5)

            def table_product(g, j, first):
                pe.wait_ge(s_xst[j], (g + 1) * 32)
                if not first:
                    by, of = j % 2, (GROUP + 1 - j % 2) // 2
                    pe.wait_ge(s_tev[by], (g - 1) * of + j // 2 + 1)
                x, p = xstage[:, j, :, :], bank(j)
                mm(p[:, 0:128], x[:, 0, :], w0a[:, 0:128], start=True, stop=True)
                mm(p[:, 160:352], x[:, 0, :], w0a[:, 160:352], start=True, stop=True)
                mm(p[:, 416:448], x[:, 0, :], w0a[:, 416:448], start=True, stop=True)
                mm(p[:, 128:160], x[0:32, 1, :], w0b[:, 64:96], start=True, stop=True)
                mm(p[:, 352:416], x[0:32, 1, :], w0b[:, 0:64], start=True, stop=True).then_inc(s_tmm, 1)

            for j in range(GROUP):
                table_product(0, j, True)
            with pe.Fori(1, GROUPS) as g:
                for j in range(GROUP):
                    table_product(g, j, False)
            pe.wait_ge(s_tev[0], GROUPS * ((GROUP + 1) // 2))
            pe.wait_ge(s_tev[1], GROUPS * (GROUP // 2))
            pe.wait_ge(s_wtab, 2)

            def radial0(s, i, j):
                pe.wait_ge(s_esc[0][j], (i + 1) * 16)
                for t in range(TPS):
                    last = mm(rad[j % 2][:, t, :], escal[:, j, t * P:(t + 1) * P], wrad[:], start=True, stop=True)
                last.then_inc(s_lin[0], 1)

            def hidden1(s, i, j):
                pe.wait_ge(s_esc[1][j], (i + 1) * 16)
                for h in range(2):
                    last = mm(hps[h * HID:(h + 1) * HID, 0:2 * P], fc1[:], escal[0:FIN, j, 2 * h * P:2 * (h + 1) * P],
                              start=True, stop=True)
                last.then_inc(s_lin[1], 1)

            def radial1(s, j):
                pe.wait_ge(s_act[1], s + 1)
                for t in (0, 2, 1, 3):
                    h = slice(t // 2 * HID, (t // 2 + 1) * HID)
                    last = mm(wps[j % 2][:, t, :], hid[h, j % 2, t % 2 * P:(t % 2 + 1) * P], fc2[h, :], start=True, stop=True)
                last.then_inc(s_w2, 1)

            def sums(l, j, b, to):
                m = (msg0, msg1)[l]
                for t in range(TPS):
                    last = mm(bank(to)[:, 0:(MSG0, MSG1)[l]], onehot[:, b, t, :], m[:, j % 2, t, :],
                              start=t == 0, stop=t == TPS - 1)
                return last

            def windows(l, s, j, more):
                pe.wait_ge(s_msg[l], s + 1)
                with pe.If(more > 0):
                    first = pe.value_load(wtab[0:1, 2, bass.ds(s, 1)], min_val=1, max_val=SUPS * NODE_TILES)
                    with pe.Fori(0, more) as k:
                        pe.wait_ge(s_ohx[l], pe.snap(first + k))
                        sums(l, j, 2, MORE).then_inc(s_aggx[l], 1)
                pe.wait_ge(s_oh[l], s + 1)
                sums(l, j, j % 2, FIRST + j % 2).then_inc(s_agg[l], 1)

            def edge_layer(l):
                for b, s_ in ((FIRST, s_agg[l]), (FIRST + 1, s_agg[l]), (MORE, s_aggx[l])):
                    mm(bank(b)[:, 0:MSG1], ident[:], zeros[:], start=True, stop=True).then_inc(s_, 1)
                if l == 0:
                    radial0(0, 0, 0)
                    radial0(1, 0, 1)
                else:
                    hidden1(0, 0, 0)
                    radial1(0, 0)
                    hidden1(1, 0, 1)

                def supertile(s, i, j, left=SUPS):
                    more = pe.value_load(wtab[0:1, 1, bass.ds(s, 1)], min_val=0, max_val=NODE_TILES - 1)
                    if l == 0:
                        if left > 2:
                            pe.wait_ge(s_msg[0], s + 1)
                            radial0(s + 2, i + (j + 2) // SLOTS, (j + 2) % SLOTS)
                    else:
                        if left > 1:
                            radial1(s + 1, (j + 1) % SLOTS)
                        if left > 2:
                            hidden1(s + 2, i + (j + 2) // SLOTS, (j + 2) % SLOTS)
                    windows(l, s, j, more)

                with pe.Fori(0, ROUNDS - 1) as i:
                    for j in range(SLOTS):
                        supertile(i * SLOTS + j, i, j)
                for j in range(SLOTS):
                    supertile((ROUNDS - 1) * SLOTS + j, ROUNDS - 1, j, SLOTS - j)

            edge_layer(0)

            def node_product0(g, first):
                def transpose(j):
                    n = g * GROUP + j
                    pe.wait_ge(s_stage[0], n + 1)
                    if j >= 2:
                        pe.wait_ge(s_hte[0], n - 1)
                    elif not first:
                        pe.wait_ge(s_hte[0], n)
                    nc.tensor.transpose(tps_[j % 2][:, 0:P], stage0[:, j, 0:P], ident[:])
                    nc.tensor.transpose(tps_[j % 2][0:MV, P:2 * P], stage0[:, j, P:DIM], ident[:]).then_inc(s_ht[0], 1)

                transpose(0)
                if not first:
                    pe.wait_ge(s_ln[0], (g - 1) * LN_STEPS[0] + 1)
                for j in range(GROUP):
                    if j + 1 < GROUP:
                        transpose(j + 1)
                    pe.wait_ge(s_hte[0], g * GROUP + j + 1)
                    mm(yps[:, j, 0:DIM], ht[:, j, 0, :], la[:], start=True, stop=False)
                    mm(yps[:, j, 0:DIM], ht[0:MV, j, 1, :], lb[:], start=False, stop=True).then_inc(s_y[0], 1)

            def features(g, first):
                for j in range(GROUP):
                    n = g * GROUP + j
                    if j == 0:
                        pe.wait_ge(s_ln[0], (g + 1) * LN_STEPS[0])
                        if not first:
                            pe.wait_ge(s_fev, n)
                    else:
                        pe.wait_ge(s_tpe, n)
                    nc.tensor.transpose(tps_[j % 2][:, 0:P], og[0][:, j, 0:P], ident[:])
                    nc.tensor.transpose(tps_[j % 2][0:MV, P:2 * P], og[0][:, j, P:DIM], ident[:]).then_inc(s_tp, 1)
                    pe.wait_ge(s_tpe, n + 1)
                    if j >= 2:
                        pe.wait_ge(s_fev, n - 1)
                    x, f = xt1[:, j, :, :], fps[j % 2]

                    mm(f[:, 0:192], x[:, 0, :], wfa[:, 0:192], start=True, stop=True)
                    mm(f[:, 224:352], x[:, 0, :], wfa[:, 224:352], start=True, stop=True)
                    mm(f[:, 192:224], x[0:32, 1, :], wfb[:, 0:32], start=True, stop=True)
                    mm(f[:, 352:384], x[0:32, 1, :], wfb[:, 32:64], start=True, stop=True).then_inc(s_f, 1)

            pe.wait_ge(s_done[0], 1)
            node_product0(0, True)
            node_product0(1, False)
            features(0, True)
            with pe.Fori(1, GROUPS - 1) as g:
                node_product0(g + 1, False)
                features(g, False)
            features(GROUPS - 1, False)

            pe.wait_ge(s_fev, GROUPS * GROUP)
            pe.wait_ge(s_ln[0], GROUPS * LN_STEPS[0])
            edge_layer(1)

            def node_product1(g, first):
                def transpose(j):
                    n = g * GROUP + j
                    pe.wait_ge(s_stage[1], n + 1)
                    if j >= 2 or not first:
                        pe.wait_ge(s_hte[1], n - (1 if j >= 2 else 0))
                    for c in range(3):
                        last = nc.tensor.transpose(tps_[j % 2][:, c * P:(c + 1) * P], stage1[:, j, c * P:(c + 1) * P], ident[:])
                    last.then_inc(s_ht[1], 1)

                transpose(0)
                if not first:
                    pe.wait_ge(s_ln[1], (g - 1) * LN_STEPS[1] + 2)
                for j in range(GROUP):
                    if j + 1 < GROUP:
                        transpose(j + 1)
                    pe.wait_ge(s_hte[1], g * GROUP + j + 1)
                    for c in range(3):
                        last = mm(yps[:, j, 0:DIM + 1], at3[:, j, c * P:(c + 1) * P], wout[:, c, :],
                                  start=c == 0, stop=c == 2)
                    last.then_inc(s_y[1], 1)

            pe.wait_ge(s_done[1], 1)
            node_product1(0, True)
            with pe.Fori(1, GROUPS) as g:
                node_product1(g, False)


def kernel(x, src, dst, edge_attr_16, edge_attr_4, node_vec1, L0_gnn_W_ss, L0_gnn_W_sv, L0_gnn_W_vs, L0_gnn_W_vv,
           L0_gnn_W_rad, L0_gnn_b_rad, L0_gnn_L_s, L0_gnn_L_v, L1_gnn_Wfc1, L1_gnn_Wfc2, L1_gnn_Wsc0, L1_gnn_Wsc1,
           L1_gnn_Wl1_0, L1_gnn_Wl1_1, L1_gnn_Wl2_s, L1_gnn_Wl2_v, L1_gnn_Wa):
    import numpy as np
    import concourse.bacc as bacc
    from concourse.bass_utils import run_bass_kernel_spmd

    (x, src, dst, ea, sh, attr, wss, wsv, wvs, wvv, wr, br, ls, lv, fc1, fc2, sc0, sc1, l10, l11, l2s, l2v, wa) = (
        np.asarray(v) for v in (
            x, src, dst, edge_attr_16, edge_attr_4, node_vec1, L0_gnn_W_ss, L0_gnn_W_sv, L0_gnn_W_vs, L0_gnn_W_vv,
            L0_gnn_W_rad, L0_gnn_b_rad, L0_gnn_L_s, L0_gnn_L_v, L1_gnn_Wfc1, L1_gnn_Wfc2, L1_gnn_Wsc0, L1_gnn_Wsc1,
            L1_gnn_Wl1_0, L1_gnn_Wl1_1, L1_gnn_Wl2_s, L1_gnn_Wl2_v, L1_gnn_Wa))

    def placed(rows, cols, *blocks):
        out = np.zeros((rows, cols), blocks[0][2].dtype)
        for r, c, b in blocks:
            out[r:r + b.shape[0], c:c + b.shape[1]] = b
        return out

    s_of = np.arange(MS)
    v_of = [MS + 3 * np.arange(MV) + d for d in range(3)]
    by_component = np.concatenate([s_of, *v_of])
    xd = placed(NODES_PAD, DIM, (0, 0, x[:, by_component]))

    def by_supertile(v, fill):
        v = v.reshape(EDGES, -1)
        v = np.concatenate([v, np.full((EDGES_PAD - EDGES, v.shape[1]), fill, v.dtype)])
        return v.reshape(SUPS, TPS, P, -1).transpose(0, 2, 1, 3).reshape(SUPS, P, -1)

    dst_pad = by_supertile(dst, NODES_PAD - 1)
    sh_pad = by_supertile(sh[:, [1, 2, 3, 0]], 0)
    dsts = np.concatenate([dst, np.full(EDGES_PAD - EDGES, NODES_PAD - 1, dst.dtype)]).reshape(ROUNDS, SLOTS, SUP_EDGES)
    V = [MS, MS + MV, MS + 2 * MV]
    wout = placed(MSG1, DIM + 1, (0, 0, l2s[:MS]), (0, DIM, wa[:MS]),
                  *((64 + 32 * d, V[d], l2v[MS:]) for d in range(3)),
                  *((160 + 64 * d, V[d], l2v[:MS]) for d in range(3)),
                  (352, 0, l2s[MS:]), (352, DIM, wa[MS:]))
    ins = {
        "xT": xd.T, "xd": xd,
        "srcs": by_supertile(src, 0),
        "dst_sh": np.concatenate([dst_pad, sh_pad.view(np.int32)], axis=2),
        "dsts": dsts,
        "escal": placed(FIN, EDGES_PAD, (0, 0, ea.T)),
        "attr": placed(NODES_PAD, 1, (0, 0, attr)).reshape(NODE_TILES, P).T,
        "w0a": placed(P, ROW0, (0, 0, wss), (64, 64, wvs), (96, 96, wvs), (64, 160, wvv), (0, 224, wsv),
                      (96, 256, wvv), (0, 320, wsv), (0, 416, wsv)),
        "w0b": placed(MV, 96, (0, 0, wvv), (0, 64, wvs)),
        "la": placed(P, DIM, (0, 0, ls), (64, V[0], lv), (96, V[1], lv)),
        "lb": placed(MV, DIM, (0, V[2], lv)),
        "wfa": placed(P, ROW1 + DIM, (64, 0, l11), (0, 32, l10), (96, 96, l11), (0, 128, l10),
                      (0, 224, sc0), (64, 288, sc1), (96, 320, sc1)),
        "wfb": placed(MV, 2 * MV, (0, 0, l11), (0, 32, sc1)),
        "wrad": np.concatenate([wr.T[:, by_component], br[None, by_component]]),
        "fc1": fc1, "fc2": np.concatenate([fc2, fc2]),
        "wout": wout.reshape(3, P, DIM + 1).transpose(1, 0, 2),
    }
    nc = bacc.Bacc("TRN2", target_bir_lowering=False, num_devices=1)
    arrays, aps = {}, {}
    for name, v in ins.items():
        v = np.ascontiguousarray(v)
        arrays[f"in_{name}"] = v
        aps[name] = nc.dram_tensor(f"in_{name}", v.shape, mybir.dt.from_np(v.dtype), kind="ExternalInput").ap()
    aps["out"] = nc.dram_tensor("out_rows", (NODES_PAD, DIM), mybir.dt.float32, kind="ExternalOutput").ap()
    mk_gnn_resnorm_d2_gnn_r8_694f30_kernel(nc, aps)
    r = run_bass_kernel_spmd(nc, [arrays], core_ids=[0])
    return r.results[0]["out_rows"][:NODES]
```

```python
import concourse.bass as bass
from concourse import mybir
from contextlib import ExitStack

NODES, EDGES = 6250, 206250
MS, MV = 64, 32
DIM = MS + 3 * MV

P = 128
TPS = 4
SUP_EDGES = TPS * P
SLOTS = 4
SUPS = -(-EDGES // (SUP_EDGES * SLOTS)) * SLOTS
ROUNDS = SUPS // SLOTS
EDGES_PAD = SUPS * SUP_EDGES

GROUP = 7
NODE_TILES = -(-NODES // P)
GROUPS = NODE_TILES // GROUP
NODES_PAD = NODE_TILES * P
assert GROUPS * GROUP == NODE_TILES

FIN = 16
SPLIT = 6 * FIN
CHUNKS = 32
CHUNK = FIN * EDGES_PAD // P // CHUNKS
assert CHUNK * CHUNKS * P == FIN * EDGES_PAD
HID = 64
ROW0 = 448
ROW1 = 224
MSG0 = DIM + 1
MSG1 = 384
WEIGHTED = 544
EPS = 1e-5
BANK = 512


def mk_gnn_resnorm_d2_gnn_r8_694f30_kernel(nc, a):
    f32, bf16, i32, i16 = mybir.dt.float32, mybir.dt.bfloat16, mybir.dt.int32, mybir.dt.int16
    ALU = mybir.AluOpType
    ACT = mybir.ActivationFunctionType
    AX = mybir.AxisListType
    ctx = ExitStack()
    with ctx:
        def sb(name, shape, dt=f32):
            return ctx.enter_context(nc.sbuf_tensor(name, shape, dt))

        def sem(name):
            return ctx.enter_context(nc.semaphore(name))

        arena = sb("arena", [P, NODE_TILES * MSG1])
        acc1 = arena[:, :].rearrange("p (w c) -> p w c", w=NODE_TILES)
        acc0 = sb("acc0", [P, NODE_TILES, MSG0])
        rows0 = arena[:, 0:SLOTS * TPS * ROW0].rearrange("p (s t c) -> p s t c", s=SLOTS, t=TPS)
        at = SLOTS * TPS * ROW0
        msg0 = arena[:, at:at + 2 * TPS * MSG0].rearrange("p (s t c) -> p s t c", s=2, t=TPS)
        at += 2 * TPS * MSG0
        rest = arena[:, at:at + 4 * CHUNK].rearrange("p (k c) -> p k c", k=4)
        parts = arena[:, at + 4 * CHUNK:at + 10 * CHUNK].bitcast(bf16).rearrange("p (k n c) -> p k n c", k=4, n=3)
        assert at + 10 * CHUNK <= NODE_TILES * MSG1
        work = sb("work", [P, TPS * (SLOTS * ROW1 + 2 * WEIGHTED + 2 * MSG1)])
        at1, at2 = SLOTS * TPS * ROW1, TPS * (SLOTS * ROW1 + 2 * WEIGHTED)
        rows1 = work[:, 0:at1].rearrange("p (s t c) -> p s t c", s=SLOTS, t=TPS)
        weighted = work[:, at1:at2].rearrange("p (s t c) -> p s t c", s=2, t=TPS)
        msg1 = work[:, at2:].rearrange("p (s t c) -> p s t c", s=2, t=TPS)

        def of_group(at, *shape):
            n = 1
            for d in shape:
                n *= d
            v = work[:, at:at + GROUP * n]
            return v.rearrange("p (g c) -> p g c", g=GROUP) if len(shape) == 1 else v.rearrange(
                "p (g h n) -> p g h n", g=GROUP, h=shape[0])

        xstage, trows = of_group(0, 2, P), of_group(GROUP * 2 * P, ROW0)
        stage0, ht, xt1, feat = (of_group(0, MSG0), of_group(1200, 2, P), of_group(3000, 2, P),
                                 of_group(4800, ROW1 + DIM))
        base_rows = of_group(4800 + GROUP * (ROW1 + DIM), DIM)
        stage1, at3 = of_group(0, MSG1), of_group(GROUP * MSG1, MSG1)

        iota = sb("iota", [P, NODES_PAD], i16)
        srcs = sb("srcs", [P, SLOTS, TPS], i32)
        dst_sh = sb("dst_sh", [P, SLOTS, 5 * TPS], i32)
        escal = sb("escal", [SPLIT + 3, SLOTS, SUP_EDGES], bf16)
        hid = sb("hid", [2 * HID, 2, 2 * P])
        onehot = sb("onehot", [P, 3, TPS, P])
        half = sb("half", [P, TPS, 2, MS])
        total = sb("total", [P, 2, TPS, DIM])
        zeros = sb("zeros", [P, MSG1])
        ident = sb("ident", [P, P])
        attr = sb("attr", [P, NODE_TILES])
        gain = sb("gain", [P, NODE_TILES])
        after = [v[:, 0:4 * GROUP * DIM].rearrange("p (k g c) -> p k g c", k=4, g=GROUP)
                 for v in (arena[:, :], acc0[:, :, :].rearrange("p w c -> p (w c)"))]
        xg, tg, sq, og = ([v[:, k] for v in after] for k in range(4))
        stat = sb("stat", [P, 8, GROUP])
        wtab = sb("wtab", [1, ROUNDS, 3, SLOTS], i32)
        wtabf = arena[0:1, SLOTS * SUP_EDGES:SLOTS * SUP_EDGES + 4 * SUPS].rearrange("p (k s) -> p k s", k=4)
        wends = sb("wends", [ROUNDS, 2, SLOTS])
        dsts = arena[0:ROUNDS, 0:SLOTS * SUP_EDGES].bitcast(i32).rearrange("p (s e) -> p s e", s=SLOTS)
        w0a, w0b = sb("w0a", [P, ROW0]), sb("w0b", [MV, 96])
        la, lb = sb("la", [P, DIM]), sb("lb", [MV, DIM])
        wfa, wfb = sb("wfa", [P, ROW1 + DIM - 2 * MV]), sb("wfb", [MV, 2 * MV])
        wedge, wedge16 = sb("wedge", [SPLIT + 3, DIM + HID]), sb("wedge16", [SPLIT + 3, DIM + HID], bf16)
        wpart1, wpart2 = sb("wpart1", [SPLIT + 3, DIM + HID], bf16), sb("wpart2", [SPLIT + 3, DIM + HID], bf16)
        fc2 = sb("fc2", [2 * HID, 192])
        wout = sb("wout", [P, 3, DIM + 1])

        ps = ctx.enter_context(nc.psum_tensor("ps", [P, 8 * BANK], f32))

        def bank(b, n=1):
            return ps[:, b * BANK:(b + n) * BANK]

        def two_to_a_bank(b, n):
            return bank(b, 2).rearrange("p (t c) -> p t c", t=TPS)[:, :, 0:n]

        rad = [two_to_a_bank(2 * b, DIM) for b in range(2)]
        wps = [two_to_a_bank(2 * b, 192) for b in range(2)]
        FIRST, MORE = 4, 6
        hps = bank(7)
        yps = bank(0, 4).rearrange("p (g c) -> p g c", c=BANK // 2)
        tps_, fps = [bank(4), bank(5)], [bank(6), bank(7)]

        def dram(name, shape):
            return nc.dram_tensor(name, shape, f32, kind="Internal").ap()

        table0, table1 = dram("table0", [NODES_PAD, ROW0]), dram("table1", [NODES_PAD, ROW1])
        split_d = nc.dram_tensor("split_d", [3, FIN, EDGES_PAD], bf16, kind="Internal").ap()
        split_rows = split_d.rearrange("n f (k c) -> n (f k) c", k=P // FIN)
        escal_rows = a["escal"].rearrange("f (k c) -> (f k) c", k=P // FIN)
        base_d, wends_d = dram("base_d", [NODES_PAD, DIM]), dram("wends_d", [2, SUPS])

        def node_rows(t, g):
            return t[bass.ds(g * (GROUP * P), GROUP * P), :].rearrange("(g p) c -> p g c", p=P)

        s_weights, s_wscaled = sem("weights_loaded"), sem("weights_scaled")
        s_const = sem("constants_made")
        s_dsts, s_ends, s_endsout, s_endsin = sem("dsts_loaded"), sem("ends_found"), sem("ends_stored"), sem("ends_loaded")
        s_wstep, s_wtab = sem("window_step"), sem("window_table_made")
        s_ein, s_split = [sem(f"chunk_loaded{k}") for k in range(4)], [sem(f"chunk_parts_stored{k}") for k in range(4)]
        s_part0, s_rest, s_part1, s_part2 = sem("part0_made"), sem("rest_made"), sem("part1_made"), sem("part2_made")
        s_wsplit, s_w16 = sem("weights_split"), sem("weight_parts_placed")
        s_zero0, s_zero1, s_acc0x = sem("sums0_zeroed"), sem("sums1_zeroed"), sem("sums0_have_x")
        s_xst = [sem(f"x_tile_loaded{j}") for j in range(GROUP)]
        s_tmm, s_tev, s_tst = sem("table0_product"), [sem("table0_by_act"), sem("table0_by_dve")], [sem(f"table0_stored{j}") for j in range(GROUP)]
        s_src = [[sem(f"srcs_loaded{l}_{j}") for j in range(SLOTS)] for l in range(2)]
        s_dsh = [[sem(f"dst_sh_loaded{l}_{j}") for j in range(SLOTS)] for l in range(2)]
        s_esc = [[sem(f"edge_scalars_loaded{l}_{j}") for j in range(SLOTS)] for l in range(2)]
        s_rows = [[sem(f"rows_gathered{l}_{j}") for j in range(SLOTS)] for l in range(2)]
        s_pool, s_sp = sem("pool_went_on"), sem("sp_went_on")
        s_lin, s_act = [sem(f"radial_product{l}") for l in range(2)], [sem(f"radial_activated{l}") for l in range(2)]
        s_w2 = sem("radial_weights")
        s_msg = [sem(f"messages_made{l}") for l in range(2)]
        s_wtd = [sem(f"rows_weighted{l}") for l in range(2)]
        s_ev2 = [sem(f"rows_weighted_by_ev2_{l}") for l in range(2)]
        s_part = [sem(f"message_part{l}") for l in range(2)]
        s_oh, s_ohx = [sem(f"first_onehot{l}") for l in range(2)], [sem(f"more_onehot{l}") for l in range(2)]
        s_agg, s_aggx = [sem(f"first_summed{l}") for l in range(2)], [sem(f"more_summed{l}") for l in range(2)]
        s_add, s_addx = [sem(f"first_added{l}") for l in range(2)], [sem(f"more_added{l}") for l in range(2)]
        s_done = [sem(f"sums_complete{l}") for l in range(2)]
        s_xin, s_xin1 = sem("x_rows_loaded"), sem("base_rows_loaded")
        s_stage, s_y = [sem(f"sums_staged{l}") for l in range(2)], [sem(f"node_product{l}") for l in range(2)]
        s_ln, s_lnact = [sem(f"norm_step{l}") for l in range(2)], [sem(f"norm_deviation{l}") for l in range(2)]
        s_ht, s_hte = [sem(f"sums_transposed{l}") for l in range(2)], [sem(f"sums_t_copied{l}") for l in range(2)]
        s_tp, s_tpe, s_f, s_fev = sem("x1_transposed"), sem("x1t_copied"), sem("features"), sem("features_copied")
        s_base, s_fst, s_out = sem("base_ready"), sem("table1_stored"), sem("out_stored")

        WEIGHTS = [(w0a, "w0a"), (w0b, "w0b"), (la, "la"), (lb, "lb"), (wfa, "wfa"), (wfb, "wfb"),
                   (wedge, "wedge"), (fc2, "fc2"), (wout, "wout"), (attr, "attr")]
        ISQ3, ISQ2 = 3.0 ** -0.5, 2.0 ** -0.5
        I8, I32, I96 = MS ** -0.5, MV ** -0.5, (MS + MV) ** -0.5
        SCALED = [(w0a[0:64, 0:64], I8 * ISQ2), (w0a[0:64, 160:448], I8 * ISQ3 * ISQ2),
                  (w0a[64:128, :], I32 * ISQ3 * ISQ2), (w0b[:], I32 * ISQ3 * ISQ2),
                  (la[0:64, :], I8), (la[64:128, :], I32), (lb[:], I32),
                  (wfa[0:64, :], I8), (wfa[64:128, :], I32), (wfb[:], I32),
                  (wedge[:, DIM:], FIN ** -0.5), (fc2[:], HID ** -0.5),
                  (wout[:, 0:2, :], I96), (wout[0:96, 2, :], I96), (wout[96:128, 2, :], I96 * ISQ3)]
        ARENA_HALF = NODE_TILES * MSG1 // 2
        LN_STEPS = [13, 12]
        block = ctx.enter_context(nc.Block())

        @block.sync
        def _(sp):
            sp.dma_start(dsts, a["dsts"]).then_inc(s_dsts, 16)
            for t, name in WEIGHTS:
                sp.dma_start(t[:], a[name]).then_inc(s_weights, 16)

            def load_x(g, j):
                at = g * (GROUP * P) + j * P
                sp.dma_start(xstage[:, j, 0, :], a["xT"][0:P, bass.ds(at, P)]).then_inc(s_xst[j], 16)
                sp.dma_start(xstage[0:MV, j, 1, :], a["xT"][P:DIM, bass.ds(at, P)]).then_inc(s_xst[j], 16)

            for j in range(GROUP):
                load_x(0, j)
            sp.dma_start(acc0[:, :, 0:DIM], a["xd"].rearrange("(w p) c -> p w c", p=P)).then_inc(s_acc0x, 16)
            sp.wait_ge(s_ends, 2)
            for e in range(2):
                sp.dma_start(wends_d[e:e + 1, :].rearrange("o (p s) -> (o p) s", s=SLOTS),
                             wends[:, e, :]).then_inc(s_endsout, 16)
            sp.wait_ge(s_endsout, 32)
            sp.dma_start(wtabf[:, 0:2, :], wends_d.rearrange("(o e) s -> o e s", o=1)).then_inc(s_endsin, 16)

            sp.wait_ge(s_wsplit, 4)
            for w, r0, r1 in ((wpart1, 3 * FIN, 5 * FIN), (wpart1, SPLIT + 1, SPLIT + 2),
                              (wpart2, 5 * FIN, 6 * FIN), (wpart2, SPLIT + 2, SPLIT + 3)):
                sp.dma_start(wedge16[r0:r1, :], w[r0:r1, :]).then_inc(s_w16, 16)

            def store_row(g, j):
                by, of = j % 2, (GROUP + 1 - j % 2) // 2
                sp.wait_ge(s_tev[by], g * of + j // 2 + 1)
                at = g * (GROUP * P) + j * P
                sp.dma_start(table0[bass.ds(at, P), :], trows[:, j, :]).then_inc(s_tst[j], 16)

            with sp.Fori(0, GROUPS - 1) as g:
                for j in range(GROUP):
                    store_row(g, j)
                    load_x(g + 1, j)
            for j in range(GROUP):
                store_row(GROUPS - 1, j)

            def load_src(l, s, j):
                sp.dma_start(srcs[:, j, :], a["srcs"][bass.ds(s, 1), :, :].rearrange("o p c -> (o p) c")).then_inc(s_src[l][j], 16)

            def load_dst_sh(l, s, j):
                sp.dma_start(dst_sh[:, j, :], a["dst_sh"][bass.ds(s, 1), :, :].rearrange("o p c -> (o p) c")).then_inc(s_dsh[l][j], 16)

            def load_escal(l, at, j):
                parts_of_s = split_d.rearrange("n f e -> (n f) e")[:, bass.ds(at, SUP_EDGES)]
                for r0, n in ((0, 3 * FIN), (3 * FIN, 2 * FIN), (5 * FIN, FIN)):
                    sp.dma_start(escal[r0:r0 + n, j, :], parts_of_s[0:n, :]).then_inc(s_esc[l][j], 16)

            for l in range(2):
                if l == 0:
                    sp.wait_ge(s_const, 4)
                    for k in range(4):
                        sp.wait_ge(s_split[k], CHUNKS // 4 * 16)
                else:
                    sp.wait_ge(s_done[0], 1)
                for j in range(SLOTS):
                    load_src(l, j, j)
                    load_escal(l, j * SUP_EDGES, j)
                    load_dst_sh(l, j, j)
                with sp.Fori(0, ROUNDS - 1) as i:
                    for j in range(SLOTS):
                        s = i * SLOTS + j
                        at = sp.snap((s + SLOTS) * SUP_EDGES)
                        sp.wait_ge(s_rows[l][j], (i + 1) * 16 * TPS)
                        load_src(l, s + SLOTS, j)
                        sp.wait_ge(s_lin[l], s + 1)
                        sp.sem_inc(s_sp, 1)
                        load_escal(l, at, j)
                        sp.wait_ge(s_msg[l], s + 2)
                        load_dst_sh(l, s + SLOTS, j)
                if l == 0:
                    sp.dma_start(xg[0], node_rows(a["xd"], 0)).then_inc(s_xin, 16)
                    def store_features(g):
                        sp.wait_ge(s_base, g + 1)
                        sp.dma_start(node_rows(table1, g), feat[:, :, 0:ROW1]).then_inc(s_fst, 16)
                        sp.dma_start(node_rows(base_d, g), base_rows).then_inc(s_fst, 16)

                    with sp.Fori(0, GROUPS - 1) as g:
                        sp.wait_ge(s_ln[0], g * LN_STEPS[0] + 1)
                        sp.dma_start(xg[0], node_rows(a["xd"], g + 1)).then_inc(s_xin, 16)
                        store_features(g)
                    store_features(GROUPS - 1)

            sp.wait_ge(s_fst, 32 * GROUPS)
            sp.wait_ge(s_ln[0], GROUPS * LN_STEPS[0])
            sp.dma_start(xg[1], node_rows(base_d, 0)).then_inc(s_xin1, 16)

            def store_out(g):
                sp.wait_ge(s_ln[1], (g + 1) * LN_STEPS[1])
                sp.dma_start(node_rows(a["out"], g), og[1]).then_inc(s_out, 16)

            with sp.Fori(0, GROUPS - 1) as g:
                sp.wait_ge(s_ln[1], g * LN_STEPS[1] + 3)
                sp.dma_start(xg[1], node_rows(base_d, g + 1)).then_inc(s_xin1, 16)
                store_out(g)
            store_out(GROUPS - 1)
            sp.wait_ge(s_out, 16 * GROUPS)

        @block.gpsimd
        def _(pool):
            def load_chunk(c, k):
                pool.dma_start(rest[:, k, :], escal_rows[:, bass.ds(c * CHUNK, CHUNK)]).then_inc(s_ein[k], 16)

            for k in range(4):
                load_chunk(k, k)
            nc.gpsimd.memset(zeros[:], 0.0).then_inc(s_const, 1)
            nc.gpsimd.memset(ident[:], 0.0).then_inc(s_const, 1)
            nc.gpsimd.memset(escal[:], 1.0).then_inc(s_const, 1)
            pool.wait_ge(s_const, 2)
            nc.gpsimd.affine_select(out=ident[:], in_=ident[:], compare_op=ALU.not_equal, fill=1.0, base=0,
                                    pattern=[[-1, P]], channel_multiplier=1).then_inc(s_const, 1)
            nc.gpsimd.iota(iota[:], pattern=[[1, NODES_PAD]], base=0, channel_multiplier=0).then_inc(s_const, 1)
            nc.gpsimd.memset(msg0[:, :, :, DIM:MSG0], 1.0).then_inc(s_zero0, 1)
            nc.gpsimd.memset(acc0[:, :, DIM:MSG0], 0.0).then_inc(s_zero0, 1)

            def store_chunk(c, k):
                pool.wait_ge(s_part2, c + 1)
                pool.sem_inc(s_pool, 1)
                pool.dma_start(split_rows[:, :, bass.ds(c * CHUNK, CHUNK)].rearrange("n p c -> p n c"),
                               parts[:, k, :, :]).then_inc(s_split[k], 16)

            with pool.Fori(0, CHUNKS // 4 - 1) as q:
                for k in range(4):
                    store_chunk(q * 4 + k, k)
                    load_chunk(q * 4 + k + 4, k)
            for k in range(4):
                store_chunk(CHUNKS - 4 + k, k)

            def gather(l, j):
                rows, table = (rows0, table0) if l == 0 else (rows1, table1)
                for t in range(TPS):
                    pool.indirect_dma_start(
                        out=rows[:, j, t, :], out_offset=None, in_=table,
                        in_offset=bass.IndirectOffsetOnAxis(ap=srcs[:, j, t:t + 1], axis=0)).then_inc(s_rows[l][j], 16)

            def gathers(l):
                for j in range(SLOTS):
                    pool.wait_ge(s_src[l][j], 16)
                    gather(l, j)
                if l == 1:
                    nc.gpsimd.memset(arena[:, ARENA_HALF:], 0.0).then_inc(s_zero1, 1)
                with pool.Fori(0, ROUNDS - 1) as i:
                    for j in range(SLOTS):
                        s = i * SLOTS + j
                        pool.wait_ge(s_wtd[l], s + 1)
                        pool.sem_inc(s_pool, 1)
                        pool.wait_ge(s_ev2[l], s + 1)
                        pool.sem_inc(s_pool, 1)
                        pool.wait_ge(s_src[l][j], (i + 2) * 16)
                        pool.sem_inc(s_pool, 1)
                        gather(l, j)

            def stage(l, g, j, first):
                if not first:
                    pool.wait_ge(s_ht[l], (g - 1) * GROUP + j + 1)
                    if l == 0 and j == 0:
                        pool.wait_ge(s_ln[0], (g - 1) * LN_STEPS[0] + 2)
                acc, to = (acc0, stage0) if l == 0 else (acc1, stage1)
                nc.gpsimd.tensor_copy(to[:, j, :], acc[:, bass.ds(g * GROUP + j, 1), :].rearrange("p o c -> p (o c)")).then_inc(s_stage[l], 1)

            for j in range(GROUP):
                pool.wait_ge(s_tst[j], 16 * GROUPS)
            gathers(0)

            pool.wait_ge(s_done[0], 1)
            for g in range(2):
                for j in range(GROUP):
                    stage(0, g, j, g == 0)

            def add_x1(g):
                pool.wait_ge(s_fev, (g + 1) * GROUP)
                pool.wait_ge(s_ln[0], (g + 1) * LN_STEPS[0])
                nc.gpsimd.tensor_tensor(base_rows[:, :, 0:P], feat[:, :, ROW1 + MV:], og[0][:, :, 0:P], ALU.add)
                nc.gpsimd.tensor_tensor(base_rows[:, :, P:DIM], feat[:, :, ROW1:ROW1 + MV], og[0][:, :, P:DIM], ALU.add).then_inc(s_base, 1)

            with pool.Fori(0, GROUPS - 2) as g:
                for j in range(GROUP):
                    stage(0, g + 2, j, False)
                add_x1(g)
            add_x1(GROUPS - 2)
            add_x1(GROUPS - 1)

            pool.wait_ge(s_fst, 32 * GROUPS)
            gathers(1)
            pool.wait_ge(s_done[1], 1)
            for j in range(GROUP):
                stage(1, 0, j, True)
            with pool.Fori(1, GROUPS) as g:
                for j in range(GROUP):
                    stage(1, g, j, False)

        @block.scalar
        def _(act):
            def table_row(g, j, first):
                act.wait_ge(s_tmm, g * GROUP + j + 1)
                if not first:
                    act.wait_ge(s_tst[j], g * 16)
                nc.scalar.activation(trows[:, j, :], bank(j)[:, 0:ROW0], ACT.Copy).then_inc(s_tev[0], 1)

            def split_four(q, first):
                split_two(q, 0, first)
                split_two(q, 2, first)

            def split_two(q, k0, first):
                for k in (k0, k0 + 1):
                    act.wait_ge(s_ein[k], (q + 1) * 16)
                    if not first:
                        act.wait_ge(s_split[k], q * 16)
                    nc.scalar.activation(parts[:, k, 0, :], rest[:, k, :], ACT.Copy).then_inc(s_part0, 1)
                for k in (k0, k0 + 1):
                    act.wait_ge(s_rest, q * 4 + k + 1)
                    nc.scalar.activation(parts[:, k, 1, :], rest[:, k, :], ACT.Copy).then_inc(s_part1, 1)

            split_four(0, True)
            for j in range(0, GROUP, 2):
                table_row(0, j, True)
            with act.Fori(1, GROUPS) as g:
                split_four(g, False)
                for j in range(0, GROUP, 2):
                    table_row(g, j, False)
            split_four(GROUPS, False)

            def weight_rows(l, s, i, j, first):
                if not first or j >= 2:
                    act.wait_ge(s_msg[l], s - 1)
                act.wait_ge(s_rows[l][j], (i + 1) * 16 * TPS)
                act.wait_ge(s_dsh[l][j], (i + 1) * 16)
                r, u = (rows0, rows1)[l][:, j, :, :], weighted[:, j % 2, :, :]
                parts = ([(0, 160, 256, 160), (1, 256, 352, 256), (3, 0, 160, 0)],
                         [(0, 0, 96, 224), (1, 32, 128, 352), (3, 0, 224, 0)])[l]
                for t in range(TPS):
                    for k, c0, c1, to in parts:
                        at = TPS + 4 * t + k
                        last = nc.scalar.activation(u[:, t, to:to + c1 - c0], r[:, t, c0:c1], ACT.Copy,
                                                    scale=dst_sh[:, j, at:at + 1].bitcast(f32))
                last.then_inc(s_wtd[l], 1)

            def supertile0(s, i, j, first):
                weight_rows(0, s, i, j, first)
                act.wait_ge(s_lin[0], s + 1)
                nc.scalar.activation(rad[j % 2], rad[j % 2], ACT.Sigmoid).then_inc(s_act[0], 1)

            for j in range(SLOTS):
                supertile0(j, 0, j, True)
            with act.Fori(1, ROUNDS) as i:
                for j in range(SLOTS):
                    supertile0(i * SLOTS + j, i, j, False)

            def deviation(l, g):
                act.wait_ge(s_ln[l], g * LN_STEPS[l] + (11, 9)[l])
                nc.scalar.activation(stat[:, 6, :], stat[:, 5, :], ACT.Sqrt).then_inc(s_lnact[l], 1)

            def transposed(l, g, norm_before=True):
                for j in range(GROUP):
                    if norm_before and j == GROUP - 2:
                        deviation(l, g - 1)
                    act.wait_ge(s_ht[l], g * GROUP + j + 1)
                    if l == 0:
                        nc.scalar.activation(ht[:, j, 0, :], tps_[j % 2][:, 0:P], ACT.Copy)
                        nc.scalar.activation(ht[0:MV, j, 1, :], tps_[j % 2][0:MV, P:2 * P], ACT.Copy).then_inc(s_hte[0], 1)
                    else:
                        nc.scalar.activation(at3[:, j, :], tps_[j % 2][:, 0:MSG1], ACT.Copy).then_inc(s_hte[1], 1)

            def features(g, first, last=False):
                if not first:
                    act.wait_ge(s_fst, g * 32)

                def transposed_x1(j):
                    act.wait_ge(s_tp, g * GROUP + j + 1)
                    nc.scalar.activation(xt1[:, j, 0, :], tps_[j % 2][:, 0:P], ACT.Copy)
                    nc.scalar.activation(xt1[0:MV, j, 1, :], tps_[j % 2][0:MV, P:2 * P], ACT.Copy).then_inc(s_tpe, 1)

                transposed_x1(0)
                for j in range(GROUP):
                    n = g * GROUP + j
                    if j + 1 < GROUP:
                        transposed_x1(j + 1)
                    elif not last:
                        deviation(0, g + 1)
                    act.wait_ge(s_f, n + 1)
                    nc.scalar.activation(feat[:, j, :], fps[j % 2][:, 0:ROW1 + DIM], ACT.Copy,
                                         scale=attr[:, bass.ds(n, 1)]).then_inc(s_fev, 1)

            transposed(0, 0, False)
            transposed(0, 1)
            features(0, True)
            with act.Fori(1, GROUPS - 1) as g:
                transposed(0, g + 1, False)
                features(g, False)
            features(GROUPS - 1, False, True)

            def silu(s, j):
                act.wait_ge(s_lin[1], s + 1)
                nc.scalar.activation(hid[:, j % 2, :], hps[:, 0:2 * P], ACT.Silu).then_inc(s_act[1], 1)

            def supertile1(s, i, j, first=False, left=SUPS):
                weight_rows(1, s, i, j, first)
                if left > 1:
                    silu(s + 1, j + 1)

            silu(0, 0)
            for j in range(SLOTS):
                supertile1(j, 0, j, first=True)
            with act.Fori(1, ROUNDS - 1) as i:
                for j in range(SLOTS):
                    supertile1(i * SLOTS + j, i, j)
            for j in range(SLOTS):
                supertile1((ROUNDS - 1) * SLOTS + j, ROUNDS - 1, j, left=SLOTS - j)

            transposed(1, 0, False)
            with act.Fori(1, GROUPS) as g:
                transposed(1, g)
            deviation(1, GROUPS - 1)

        @block.vector
        def _(dve):
            dve.wait_ge(s_dsts, 16)
            nc.vector.tensor_reduce(wends[:, 0, :], dsts, AX.X, ALU.min).then_inc(s_ends, 1)
            nc.vector.tensor_reduce(wends[:, 1, :], dsts, AX.X, ALU.max).then_inc(s_ends, 1)
            def split_four(q):
                split_two(q, 0)
                split_two(q, 2)

            def split_two(q, k0):
                for k in (k0, k0 + 1):
                    dve.wait_ge(s_part0, q * 4 + k + 1)
                    nc.vector.tensor_tensor(rest[:, k, :], rest[:, k, :], parts[:, k, 0, :], ALU.subtract).then_inc(s_rest, 1)
                for k in (k0, k0 + 1):
                    dve.wait_ge(s_part1, q * 4 + k + 1)
                    nc.vector.tensor_tensor(parts[:, k, 2, :], rest[:, k, :], parts[:, k, 1, :], ALU.subtract).then_inc(s_part2, 1)

            assert CHUNKS == 4 * (GROUPS + 1)
            split_four(0)
            dve.wait_ge(s_weights, 16 * len(WEIGHTS))
            for w, c in SCALED:
                nc.vector.tensor_scalar(w, w, c, None, ALU.mult).then_inc(s_wscaled, 1)
            dve.wait_ge(s_wscaled, len(SCALED))
            nc.vector.tensor_copy(wedge16[:], wedge[:]).then_inc(s_wsplit, 1)
            dve.wait_ge(s_wsplit, 1)
            nc.vector.tensor_tensor(wedge[:], wedge[:], wedge16[:], ALU.subtract).then_inc(s_wsplit, 1)
            dve.wait_ge(s_wsplit, 2)
            nc.vector.tensor_copy(wpart1[:], wedge[:]).then_inc(s_wsplit, 1)
            dve.wait_ge(s_wsplit, 3)
            nc.vector.tensor_tensor(wpart2[:], wedge[:], wpart1[:], ALU.subtract).then_inc(s_wsplit, 1)
            dve.wait_ge(s_endsin, 16)
            ends, endsf = wtab[:, :, 0:2, :].rearrange("p i k j -> p k i j"), wtabf[:, 0:2, :].rearrange("p k (i j) -> p k i j", j=SLOTS)
            nc.vector.tensor_copy(ends, endsf).then_inc(s_wstep, 1)
            dve.wait_ge(s_wstep, 1)
            nc.vector.tensor_scalar(ends, ends, P.bit_length() - 1, None,
                                    ALU.arith_shift_right).then_inc(s_wstep, 1)
            dve.wait_ge(s_wstep, 2)
            nc.vector.tensor_copy(endsf, ends).then_inc(s_wstep, 1)
            dve.wait_ge(s_wstep, 3)
            nc.vector.tensor_tensor(wtabf[:, 1, :], wtabf[:, 1, :], wtabf[:, 0, :], ALU.subtract).then_inc(s_wstep, 1)
            dve.wait_ge(s_wstep, 4)
            nc.vector.tensor_tensor_scan(wtabf[:, 2, :], wtabf[:, 1, :], wtabf[:, 1, :], 1.0,
                                         ALU.add, ALU.bypass).then_inc(s_wstep, 1)
            dve.wait_ge(s_wstep, 5)
            nc.vector.tensor_tensor(wtabf[:, 3, :], wtabf[:, 2, :], wtabf[:, 1, :], ALU.subtract).then_inc(s_wstep, 1)
            dve.wait_ge(s_wstep, 6)
            nc.vector.tensor_copy(wtab[:, :, 1, :], wtabf[:, 1, :].rearrange("p (i j) -> p i j", j=SLOTS)).then_inc(s_wtab, 1)
            nc.vector.tensor_copy(wtab[:, :, 2, :], wtabf[:, 3, :].rearrange("p (i j) -> p i j", j=SLOTS)).then_inc(s_wtab, 1)

            def table_row(g, j, first):
                dve.wait_ge(s_tmm, g * GROUP + j + 1)
                if not first:
                    dve.wait_ge(s_tst[j], g * 16)
                nc.vector.tensor_copy(trows[:, j, :], bank(j)[:, 0:ROW0]).then_inc(s_tev[1], 1)

            for j in range(1, GROUP, 2):
                table_row(0, j, True)
            with dve.Fori(1, GROUPS) as g:
                split_four(g)
                for j in range(1, GROUP, 2):
                    table_row(g, j, False)
            split_four(GROUPS)

            def bc(x, axis, shape):
                return x.unsqueeze(axis).to_broadcast(shape)

            def weight_by_ev2(l, s, i, j):
                dve.wait_ge(s_rows[l][j], (i + 1) * 16 * TPS)
                dve.wait_ge(s_dsh[l][j], (i + 1) * 16)
                r, (c0, to) = (rows0, rows1)[l], ((352, 352), (128, 448))[l]
                ev2 = dst_sh[:, j, TPS:].bitcast(f32).rearrange("p (t k) -> p t k", k=4)[:, :, 2]
                nc.vector.tensor_tensor(weighted[:, j % 2, :, to:to + 96], r[:, j, :, c0:c0 + 96],
                                        bc(ev2, 2, [P, TPS, 96]), ALU.mult).then_inc(s_ev2[l], 1)

            def messages0(s, j):
                u, m, c, h, a = weighted[:, j % 2, :, :], msg0[:, j % 2, :, :], rad[j % 2], half, total[:, j % 2, :, :]

                def blocks(x, n):
                    return x.rearrange("p t (k c) -> p t k c", k=n)

                dve.wait_ge(s_ev2[0], s + 1)
                dve.wait_ge(s_wtd[0], s + 1)
                nc.vector.tensor_tensor(h[:], blocks(u[:, :, 0:512], 2)[:, :, :, 0:MS],
                                        blocks(u[:, :, 160:544], 2)[:, :, :, 0:MS], ALU.add).then_inc(s_part[0], 1)
                nc.vector.tensor_tensor(blocks(a[:, :, MS:DIM], 3), blocks(u[:, :, MS:DIM], 3),
                                        blocks(u[:, :, 160:448], 3)[:, :, :, MS:96], ALU.add).then_inc(s_part[0], 1)
                dve.wait_ge(s_part[0], s * 3 + 1)
                nc.vector.tensor_tensor(a[:, :, 0:MS], h[:, :, 0, :], h[:, :, 1, :], ALU.add).then_inc(s_part[0], 1)
                dve.wait_ge(s_part[0], s * 3 + 3)
                dve.wait_ge(s_act[0], s + 1)
                nc.vector.tensor_tensor(m[:, :, 0:DIM], a, c, ALU.mult).then_inc(s_msg[0], 1)

            def messages1(s, j):
                u, m, w, h = weighted[:, j % 2, :, :], msg1[:, j % 2, :, :], wps[j % 2], half

                def blocks(x, n):
                    return x.rearrange("p t (k c) -> p t k c", k=n)

                dve.wait_ge(s_ev2[1], s + 1)
                dve.wait_ge(s_wtd[1], s + 1)
                nc.vector.tensor_tensor(h[:, :, 0, 0:MV], u[:, :, 224:256], u[:, :, 416:448], ALU.add).then_inc(s_part[1], 1)
                dve.wait_ge(s_w2, s + 1)
                nc.vector.tensor_tensor(m[:, :, 0:MS], u[:, :, 32:96], w[:, :, 0:64], ALU.mult)
                nc.vector.tensor_tensor(blocks(m[:, :, 64:160], 3), blocks(u[:, :, 0:288], 3)[:, :, :, 0:MV],
                                        bc(w[:, :, 128:160], 2, [P, TPS, 3, MV]), ALU.mult)
                dve.wait_ge(s_part[1], s * 2 + 1)
                nc.vector.tensor_tensor(h[:, :, 1, 0:MV], h[:, :, 0, 0:MV], u[:, :, 512:544], ALU.add).then_inc(s_part[1], 1)
                nc.vector.tensor_tensor(blocks(m[:, :, 160:352], 3), blocks(u[:, :, 256:544], 3)[:, :, :, 0:MS],
                                        bc(w[:, :, 64:128], 2, [P, TPS, 3, MS]), ALU.mult)
                dve.wait_ge(s_part[1], s * 2 + 2)
                nc.vector.tensor_tensor(m[:, :, 352:384], h[:, :, 1, 0:MV], w[:, :, 160:192], ALU.mult).then_inc(s_msg[1], 1)

            def select(j, b, window):
                return nc.vector.tensor_tensor(onehot[:, b, :, :], bc(iota[:, bass.ds(window * P, P)], 1, [P, TPS, P]),
                                               bc(dst_sh[:, j, 0:TPS], 2, [P, TPS, P]), ALU.is_equal)

            def add_sums(l, b, window):
                acc, n = (acc0, MSG0) if l == 0 else (acc1, MSG1)
                to = acc[:, bass.ds(window, 1), :].rearrange("p o c -> p (o c)")
                return nc.vector.tensor_tensor(to, to, bank(b)[:, 0:n], ALU.add)

            def edge_layer(l):
                LAST = NODE_TILES - 1
                waiting, newer = dve.alloc_register(f"window_to_add{l}"), dve.alloc_register(f"window_after{l}")
                waiting_more = dve.alloc_register(f"more_to_add{l}")

                def held(register):
                    return dve.snap(register, min_val=0, max_val=LAST)

                dve.reg_mov(waiting, 0)
                dve.reg_mov(newer, 0)
                dve.reg_mov(waiting_more, 0)
                dve.sem_inc(s_add[l], 1)
                dve.sem_inc(s_addx[l], 1)

                def supertile(s, i, j, window, more):
                    dve.wait_ge(s_agg[l], s + 1)
                    dve.wait_ge(s_add[l], s + 1)
                    add_sums(l, FIRST + j % 2, held(waiting)).then_inc(s_add[l], 1)
                    weight_by_ev2(l, s, i, j)
                    select(j, j % 2, window).then_inc(s_oh[l], 1)
                    (messages0, messages1)[l](s, j)
                    with dve.If(more > 0):
                        first = dve.value_load(wtab[0:1, bass.ds(i, 1), 2, j:j + 1], min_val=1, max_val=SUPS * NODE_TILES)
                        with dve.Fori(0, more) as k:
                            e = dve.snap(first + k)
                            dve.wait_ge(s_aggx[l], e)
                            dve.wait_ge(s_addx[l], e)
                            dve.wait_ge(s_add[l], s + 2)
                            add_sums(l, MORE, held(waiting_more)).then_inc(s_addx[l], 1)
                            at = dve.snap(window + k + 1).with_bounds(min_val=1, max_val=LAST)
                            dve.wait_ge(s_addx[l], e + 1)
                            select(j, 2, at).then_inc(s_ohx[l], 1)
                            dve.reg_mov(waiting_more, at)
                    dve.reg_mov(waiting, held(newer))
                    dve.reg_mov(newer, window)

                with dve.Fori(0, ROUNDS) as i:
                    _, values = nc.values_load_multi_w_load_instructions(
                        wtab[0:1, bass.ds(i, 1), 0:2, :], engines=[dve.engine], min_val=0, max_val=LAST,
                        skip_runtime_bounds_check_because="a dst is a node's number, so its window is one of the tiles")
                    for j in range(SLOTS):
                        supertile(i * SLOTS + j, i, j, values[j], values[SLOTS + j])
                for k, window in enumerate((waiting, newer)):
                    dve.wait_ge(s_agg[l], SUPS + k + 1)
                    dve.wait_ge(s_add[l], SUPS + k + 1)
                    add_sums(l, FIRST + k, held(window)).then_inc(s_add[l], 1)
                first = dve.value_load(wtab[0:1, ROUNDS - 1, 2, SLOTS - 1:SLOTS], min_val=1, max_val=SUPS * NODE_TILES)
                more = dve.value_load(wtab[0:1, ROUNDS - 1, 1, SLOTS - 1:SLOTS], min_val=0, max_val=LAST)
                e = dve.snap(first + more)
                dve.wait_ge(s_aggx[l], e)
                dve.wait_ge(s_addx[l], e)
                dve.wait_ge(s_add[l], SUPS + 3)
                add_sums(l, MORE, held(waiting_more)).then_inc(s_addx[l], 1)
                dve.wait_ge(s_addx[l], e + 1)
                dve.sem_inc(s_done[l], 1)

            dve.wait_ge(s_const, 5)
            dve.wait_ge(s_zero0, 2)
            dve.wait_ge(s_acc0x, 16)
            dve.wait_ge(s_wtab, 2)
            edge_layer(0)

            def norm(l, g, n):
                base = g * LN_STEPS[l] + n
                dve.wait_ge(s_ln[l], base)
                nc.vector.tensor_reduce(stat[:, 3, :], tg[l], AX.X, ALU.add, negate=True).then_inc(s_ln[l], 1)
                dve.wait_ge(s_ln[l], base + 1)
                nc.vector.tensor_scalar(stat[:, 4, :], stat[:, 3, :], 1.0 / DIM, None, ALU.mult).then_inc(s_ln[l], 1)
                dve.wait_ge(s_ln[l], base + 2)
                nc.vector.tensor_tensor(tg[l], tg[l], bc(stat[:, 4, :], 2, [P, GROUP, DIM]), ALU.add).then_inc(s_ln[l], 1)
                dve.wait_ge(s_ln[l], base + 3)
                nc.vector.tensor_tensor(sq[l], tg[l], tg[l], ALU.mult).then_inc(s_ln[l], 1)
                dve.wait_ge(s_ln[l], base + 4)
                nc.vector.tensor_reduce(stat[:, 0, :], sq[l], AX.X, ALU.add).then_inc(s_ln[l], 1)
                dve.wait_ge(s_ln[l], base + 5)
                nc.vector.tensor_scalar(stat[:, 5, :], stat[:, 0, :], 1.0 / DIM, EPS, ALU.mult, ALU.add).then_inc(s_ln[l], 1)
                dve.wait_ge(s_lnact[l], g + 1)
                nc.vector.reciprocal(stat[:, 7, :], stat[:, 6, :]).then_inc(s_ln[l], 1)
                dve.wait_ge(s_ln[l], base + 7)

            def nodes0(g, first):
                base = g * LN_STEPS[0]
                dve.wait_ge(s_y[0], (g + 1) * GROUP)
                dve.wait_ge(s_xin, (g + 1) * 16)
                if not first:
                    dve.wait_ge(s_ln[0], base)
                nc.vector.tensor_tensor(tg[0], yps[:, 0:GROUP, 0:DIM], xg[0], ALU.add).then_inc(s_ln[0], 1)
                dve.wait_ge(s_stage[0], (g + 1) * GROUP)
                nc.vector.tensor_scalar(stat[:, 0, :], stage0[:, :, DIM], 1.0, None, ALU.max).then_inc(s_ln[0], 1)
                dve.wait_ge(s_ln[0], base + 2)
                nc.vector.reciprocal(stat[:, 1, :], stat[:, 0, :]).then_inc(s_ln[0], 1)
                dve.wait_ge(s_ln[0], base + 3)
                nc.vector.tensor_tensor(stat[:, 2, :], stat[:, 1, :], attr[:, bass.ds(g * GROUP, GROUP)], ALU.mult).then_inc(s_ln[0], 1)
                dve.wait_ge(s_ln[0], base + 4)
                nc.vector.tensor_tensor(gain[:, bass.ds(g * GROUP, GROUP)], stat[:, 2, :], stat[:, 2, :], ALU.mult).then_inc(s_ln[0], 1)
                norm(0, g, 5)
                if not first:
                    dve.wait_ge(s_base, g)
                nc.vector.tensor_tensor(og[0], tg[0], bc(stat[:, 7, :], 2, [P, GROUP, DIM]), ALU.mult).then_inc(s_ln[0], 1)

            nodes0(0, True)
            with dve.Fori(1, GROUPS) as g:
                nodes0(g, False)

            dve.wait_ge(s_stage[0], GROUPS * GROUP)
            dve.wait_ge(s_fst, 32 * GROUPS)
            nc.vector.memset(arena[:, 0:ARENA_HALF], 0.0).then_inc(s_zero1, 1)
            dve.wait_ge(s_zero1, 2)
            edge_layer(1)

            def nodes1(g, first):
                base = g * LN_STEPS[1]
                dve.wait_ge(s_y[1], (g + 1) * GROUP)
                if not first:
                    dve.wait_ge(s_ln[1], base)
                nc.vector.tensor_tensor(stat[:, 0, :], yps[:, 0:GROUP, DIM], gain[:, bass.ds(g * GROUP, GROUP)], ALU.mult).then_inc(s_ln[1], 1)
                dve.wait_ge(s_ln[1], base + 1)
                nc.vector.tensor_tensor(tg[1], yps[:, 0:GROUP, 0:DIM], bc(stat[:, 0, :], 2, [P, GROUP, DIM]), ALU.mult).then_inc(s_ln[1], 1)
                dve.wait_ge(s_xin1, (g + 1) * 16)
                dve.wait_ge(s_ln[1], base + 2)
                nc.vector.tensor_tensor(tg[1], tg[1], xg[1], ALU.add).then_inc(s_ln[1], 1)
                norm(1, g, 3)
                if not first:
                    dve.wait_ge(s_out, g * 16)
                nc.vector.tensor_tensor(og[1][:, :, 0:MS], tg[1][:, :, 0:MS], bc(stat[:, 7, :], 2, [P, GROUP, MS]), ALU.mult).then_inc(s_ln[1], 1)
                nc.vector.tensor_tensor(og[1][:, :, MS:DIM].rearrange("p g (v d) -> p g d v", d=3),
                                        tg[1][:, :, MS:DIM].rearrange("p g (d v) -> p g d v", d=3),
                                        bc(stat[:, 7, :].unsqueeze(2), 3, [P, GROUP, 3, MV]), ALU.mult).then_inc(s_ln[1], 1)

            nodes1(0, True)
            with dve.Fori(1, GROUPS) as g:
                nodes1(g, False)

        @block.tensor
        def _(pe):
            mm = nc.tensor.matmul
            pe.wait_ge(s_wscaled, len(SCALED))
            pe.wait_ge(s_const, 5)

            def table_product(g, j, first):
                pe.wait_ge(s_xst[j], (g + 1) * 32)
                if not first:
                    by, of = j % 2, (GROUP + 1 - j % 2) // 2
                    pe.wait_ge(s_tev[by], (g - 1) * of + j // 2 + 1)
                x, p = xstage[:, j, :, :], bank(j)
                mm(p[:, 0:128], x[:, 0, :], w0a[:, 0:128], start=True, stop=True)
                mm(p[:, 160:352], x[:, 0, :], w0a[:, 160:352], start=True, stop=True)
                mm(p[:, 416:448], x[:, 0, :], w0a[:, 416:448], start=True, stop=True)
                mm(p[:, 128:160], x[0:32, 1, :], w0b[:, 64:96], start=True, stop=True)
                mm(p[:, 352:416], x[0:32, 1, :], w0b[:, 0:64], start=True, stop=True).then_inc(s_tmm, 1)

            for j in range(GROUP):
                table_product(0, j, True)
            with pe.Fori(1, GROUPS) as g:
                for j in range(GROUP):
                    table_product(g, j, False)
            pe.wait_ge(s_tev[0], GROUPS * ((GROUP + 1) // 2))
            pe.wait_ge(s_tev[1], GROUPS * (GROUP // 2))
            pe.wait_ge(s_wtab, 2)
            pe.wait_ge(s_w16, 64)

            def radial0(s, i, j):
                pe.wait_ge(s_esc[0][j], (i + 1) * 48)
                for t in range(TPS):
                    last = mm(rad[j % 2][:, t, :], escal[:, j, t * P:(t + 1) * P], wedge16[:, 0:DIM], start=True, stop=True)
                last.then_inc(s_lin[0], 1)

            def hidden1(s, i, j):
                pe.wait_ge(s_esc[1][j], (i + 1) * 48)
                for h in range(2):
                    last = mm(hps[h * HID:(h + 1) * HID, 0:2 * P], wedge16[0:SPLIT, DIM:],
                              escal[0:SPLIT, j, 2 * h * P:2 * (h + 1) * P], start=True, stop=True)
                last.then_inc(s_lin[1], 1)

            def radial1(s, j):
                pe.wait_ge(s_act[1], s + 1)
                for t in (0, 2, 1, 3):
                    h = slice(t // 2 * HID, (t // 2 + 1) * HID)
                    last = mm(wps[j % 2][:, t, :], hid[h, j % 2, t % 2 * P:(t % 2 + 1) * P], fc2[h, :], start=True, stop=True)
                last.then_inc(s_w2, 1)

            def sums(l, j, b, to):
                m = (msg0, msg1)[l]
                for t in range(TPS):
                    last = mm(bank(to)[:, 0:(MSG0, MSG1)[l]], onehot[:, b, t, :], m[:, j % 2, t, :],
                              start=t == 0, stop=t == TPS - 1)
                return last

            def windows(l, s, i, j, more):
                pe.wait_ge(s_msg[l], s + 1)
                with pe.If(more > 0):
                    first = pe.value_load(wtab[0:1, bass.ds(i, 1), 2, j:j + 1], min_val=1, max_val=SUPS * NODE_TILES)
                    with pe.Fori(0, more) as k:
                        pe.wait_ge(s_ohx[l], pe.snap(first + k))
                        sums(l, j, 2, MORE).then_inc(s_aggx[l], 1)
                pe.wait_ge(s_oh[l], s + 1)
                sums(l, j, j % 2, FIRST + j % 2).then_inc(s_agg[l], 1)

            def edge_layer(l):
                for b, s_ in ((FIRST, s_agg[l]), (FIRST + 1, s_agg[l]), (MORE, s_aggx[l])):
                    mm(bank(b)[:, 0:MSG1], ident[:], zeros[:], start=True, stop=True).then_inc(s_, 1)
                if l == 0:
                    radial0(0, 0, 0)
                    radial0(1, 0, 1)
                else:
                    hidden1(0, 0, 0)
                    radial1(0, 0)
                    hidden1(1, 0, 1)

                def supertile(s, i, j, more, left=SUPS):
                    if l == 0:
                        if left > 2:
                            pe.wait_ge(s_msg[0], s + 1)
                            radial0(s + 2, i + (j + 2) // SLOTS, (j + 2) % SLOTS)
                    else:
                        if left > 1:
                            radial1(s + 1, (j + 1) % SLOTS)
                        if left > 2:
                            hidden1(s + 2, i + (j + 2) // SLOTS, (j + 2) % SLOTS)
                    windows(l, s, i, j, more)

                def further_windows(i):
                    return nc.values_load_multi_w_load_instructions(
                        wtab[0:1, bass.ds(i, 1), 1, :], engines=[pe.engine], min_val=0, max_val=NODE_TILES - 1,
                        skip_runtime_bounds_check_because="a dst is a node's number, so its window is one of the tiles")[1]

                with pe.Fori(0, ROUNDS - 1) as i:
                    more = further_windows(i)
                    for j in range(SLOTS):
                        supertile(i * SLOTS + j, i, j, more[j])
                more = further_windows(ROUNDS - 1)
                for j in range(SLOTS):
                    supertile((ROUNDS - 1) * SLOTS + j, ROUNDS - 1, j, more[j], SLOTS - j)

            edge_layer(0)

            def node_product0(g, first):
                def transpose(j):
                    n = g * GROUP + j
                    pe.wait_ge(s_stage[0], n + 1)
                    if j >= 2:
                        pe.wait_ge(s_hte[0], n - 1)
                    elif not first:
                        pe.wait_ge(s_hte[0], n)
                    nc.tensor.transpose(tps_[j % 2][:, 0:P], stage0[:, j, 0:P], ident[:])
                    nc.tensor.transpose(tps_[j % 2][0:MV, P:2 * P], stage0[:, j, P:DIM], ident[:]).then_inc(s_ht[0], 1)

                transpose(0)
                if not first:
                    pe.wait_ge(s_ln[0], (g - 1) * LN_STEPS[0] + 1)
                for j in range(GROUP):
                    if j + 1 < GROUP:
                        transpose(j + 1)
                    pe.wait_ge(s_hte[0], g * GROUP + j + 1)
                    mm(yps[:, j, 0:DIM], ht[:, j, 0, :], la[:], start=True, stop=False)
                    mm(yps[:, j, 0:DIM], ht[0:MV, j, 1, :], lb[:], start=False, stop=True).then_inc(s_y[0], 1)

            def features(g, first):
                def transpose(j):
                    if j >= 2:
                        pe.wait_ge(s_tpe, g * GROUP + j - 1)
                    nc.tensor.transpose(tps_[j % 2][:, 0:P], og[0][:, j, 0:P], ident[:])
                    nc.tensor.transpose(tps_[j % 2][0:MV, P:2 * P], og[0][:, j, P:DIM], ident[:]).then_inc(s_tp, 1)

                pe.wait_ge(s_ln[0], (g + 1) * LN_STEPS[0])
                transpose(0)
                if not first:
                    pe.wait_ge(s_fev, g * GROUP)
                for j in range(GROUP):
                    n = g * GROUP + j
                    if j + 1 < GROUP:
                        transpose(j + 1)
                    pe.wait_ge(s_tpe, n + 1)
                    if j >= 2:
                        pe.wait_ge(s_fev, n - 1)
                    x, f = xt1[:, j, :, :], fps[j % 2]
                    mm(f[:, 0:192], x[:, 0, :], wfa[:, 0:192], start=True, stop=True)
                    mm(f[:, 256:384], x[:, 0, :], wfa[:, 192:320], start=True, stop=True)
                    mm(f[:, 192:256], x[0:MV, 1, :], wfb[:], start=True, stop=True).then_inc(s_f, 1)

            pe.wait_ge(s_done[0], 1)
            node_product0(0, True)
            node_product0(1, False)
            features(0, True)
            with pe.Fori(1, GROUPS - 1) as g:
                node_product0(g + 1, False)
                features(g, False)
            features(GROUPS - 1, False)

            pe.wait_ge(s_fev, GROUPS * GROUP)
            pe.wait_ge(s_ln[0], GROUPS * LN_STEPS[0])
            edge_layer(1)

            def node_product1(g, first):
                def transpose(j):
                    n = g * GROUP + j
                    pe.wait_ge(s_stage[1], n + 1)
                    if j >= 2 or not first:
                        pe.wait_ge(s_hte[1], n - (1 if j >= 2 else 0))
                    for c in range(3):
                        last = nc.tensor.transpose(tps_[j % 2][:, c * P:(c + 1) * P], stage1[:, j, c * P:(c + 1) * P], ident[:])
                    last.then_inc(s_ht[1], 1)

                transpose(0)
                if not first:
                    pe.wait_ge(s_ln[1], (g - 1) * LN_STEPS[1] + 2)
                for j in range(GROUP):
                    if j + 1 < GROUP:
                        transpose(j + 1)
                    pe.wait_ge(s_hte[1], g * GROUP + j + 1)
                    for c in range(3):
                        last = mm(yps[:, j, 0:DIM + 1], at3[:, j, c * P:(c + 1) * P], wout[:, c, :],
                                  start=c == 0, stop=c == 2)
                    last.then_inc(s_y[1], 1)

            pe.wait_ge(s_done[1], 1)
            node_product1(0, True)
            with pe.Fori(1, GROUPS) as g:
                node_product1(g, False)


def kernel(x, src, dst, edge_attr_16, edge_attr_4, node_vec1, L0_gnn_W_ss, L0_gnn_W_sv, L0_gnn_W_vs, L0_gnn_W_vv,
           L0_gnn_W_rad, L0_gnn_b_rad, L0_gnn_L_s, L0_gnn_L_v, L1_gnn_Wfc1, L1_gnn_Wfc2, L1_gnn_Wsc0, L1_gnn_Wsc1,
           L1_gnn_Wl1_0, L1_gnn_Wl1_1, L1_gnn_Wl2_s, L1_gnn_Wl2_v, L1_gnn_Wa):
    import numpy as np
    import concourse.bacc as bacc
    from concourse.bass_utils import run_bass_kernel_spmd

    (x, src, dst, ea, sh, attr, wss, wsv, wvs, wvv, wr, br, ls, lv, fc1, fc2, sc0, sc1, l10, l11, l2s, l2v, wa) = (
        np.asarray(v) for v in (
            x, src, dst, edge_attr_16, edge_attr_4, node_vec1, L0_gnn_W_ss, L0_gnn_W_sv, L0_gnn_W_vs, L0_gnn_W_vv,
            L0_gnn_W_rad, L0_gnn_b_rad, L0_gnn_L_s, L0_gnn_L_v, L1_gnn_Wfc1, L1_gnn_Wfc2, L1_gnn_Wsc0, L1_gnn_Wsc1,
            L1_gnn_Wl1_0, L1_gnn_Wl1_1, L1_gnn_Wl2_s, L1_gnn_Wl2_v, L1_gnn_Wa))

    def placed(rows, cols, *blocks):
        out = np.zeros((rows, cols), blocks[0][2].dtype)
        for r, c, b in blocks:
            out[r:r + b.shape[0], c:c + b.shape[1]] = b
        return out

    s_of = np.arange(MS)
    v_of = [MS + 3 * np.arange(MV) + d for d in range(3)]
    by_component = np.concatenate([s_of, *v_of])
    xd = placed(NODES_PAD, DIM, (0, 0, x[:, by_component]))

    def by_supertile(v, fill):
        v = v.reshape(EDGES, -1)
        v = np.concatenate([v, np.full((EDGES_PAD - EDGES, v.shape[1]), fill, v.dtype)])
        return v.reshape(SUPS, TPS, P, -1).transpose(0, 2, 1, 3).reshape(SUPS, P, -1)

    dst_pad = by_supertile(dst, NODES_PAD - 1)
    sh_pad = by_supertile(sh[:, [1, 2, 3, 0]], 0)
    dsts = np.concatenate([dst, np.full(EDGES_PAD - EDGES, NODES_PAD - 1, dst.dtype)]).reshape(ROUNDS, SLOTS, SUP_EDGES)
    V = [MS, MS + MV, MS + 2 * MV]
    wout = placed(MSG1, DIM + 1, (0, 0, l2s[:MS]), (0, DIM, wa[:MS]),
                  *((64 + 32 * d, V[d], l2v[MS:]) for d in range(3)),
                  *((160 + 64 * d, V[d], l2v[:MS]) for d in range(3)),
                  (352, 0, l2s[MS:]), (352, DIM, wa[MS:]))
    ins = {
        "xT": xd.T, "xd": xd,
        "srcs": by_supertile(src, 0),
        "dst_sh": np.concatenate([dst_pad, sh_pad.view(np.int32)], axis=2),
        "dsts": dsts,
        "escal": placed(FIN, EDGES_PAD, (0, 0, ea.T)),
        "attr": placed(NODES_PAD, 1, (0, 0, attr)).reshape(NODE_TILES, P).T,
        "w0a": placed(P, ROW0, (0, 0, wss), (64, 64, wvs), (96, 96, wvs), (64, 160, wvv), (0, 224, wsv),
                      (96, 256, wvv), (0, 320, wsv), (0, 416, wsv)),
        "w0b": placed(MV, 96, (0, 0, wvv), (0, 64, wvs)),
        "la": placed(P, DIM, (0, 0, ls), (64, V[0], lv), (96, V[1], lv)),
        "lb": placed(MV, DIM, (0, V[2], lv)),
        "wfa": placed(P, ROW1 + DIM - 2 * MV, (64, 0, l11), (0, 32, l10), (96, 96, l11), (0, 128, l10),
                      (0, 192, sc0), (64, 256, sc1), (96, 288, sc1)),
        "wfb": placed(MV, 2 * MV, (0, 0, l11), (0, 32, sc1)),
        "wedge": placed(SPLIT + 3, DIM + HID, *((k * FIN, 0, wr.T[:, by_component]) for k in range(6)),
                        *((k * FIN, DIM, fc1) for k in range(6)),
                        *((SPLIT + k, 0, br[None, by_component]) for k in range(3))),
        "fc2": np.concatenate([fc2, fc2]),
        "wout": wout.reshape(3, P, DIM + 1).transpose(1, 0, 2),
    }
    nc = bacc.Bacc("TRN2", target_bir_lowering=False, num_devices=1)
    arrays, aps = {}, {}
    for name, v in ins.items():
        v = np.ascontiguousarray(v)
        arrays[f"in_{name}"] = v
        aps[name] = nc.dram_tensor(f"in_{name}", v.shape, mybir.dt.from_np(v.dtype), kind="ExternalInput").ap()
    aps["out"] = nc.dram_tensor("out_rows", (NODES_PAD, DIM), mybir.dt.float32, kind="ExternalOutput").ap()
    mk_gnn_resnorm_d2_gnn_r8_694f30_kernel(nc, aps)
    r = run_bass_kernel_spmd(nc, [arrays], core_ids=[0])
    return r.results[0]["out_rows"][:NODES]
```
